# Optimizing a Trainium2 kernel written in Bass

```python
import numpy as np
import jax
import jax.numpy as jnp

def _softmax(x, axis=-1):
    return jax.nn.softmax(x, axis=axis)

def _gelu(x):
    return jax.nn.gelu(x, approximate=True)

def _silu(x):
    return jax.nn.silu(x)

def _sigmoid(x):
    return jax.nn.sigmoid(x)

def _layernorm(x, axis=-1, eps=1e-05):
    m = jnp.mean(x, axis=axis, keepdims=True)
    v = jnp.var(x, axis=axis, keepdims=True)
    return (x - m) / jnp.sqrt(v + eps)

def _scatter_add(tgt, idx, src, axis=0):
    return tgt.at[idx].add(src)

def _segment_sum(src, seg, n):
    return jax.ops.segment_sum(src, seg, n)
kernel_name = 'mk_seq_preln_d1_jaxref_r8_09df77'

def setup_inputs(seed: int=0):
    np.random.seed(seed)
    _w = jnp.asarray

    def _L0_attn_setup():
        import jax, jax.numpy as jnp
        import numpy as np
        HIDDEN = 512
        HEADS = 32
        D_K = HIDDEN // HEADS
        key = jax.random.key(seed)
        ks = jax.random.split(key, 5)
        scale = 1.0 / np.sqrt(HIDDEN)
        x = jax.random.normal(ks[0], (2, 256, HIDDEN), dtype=jnp.float32)
        w_q = jax.random.uniform(ks[1], (HIDDEN, HIDDEN), jnp.float32, -scale, scale)
        w_k = jax.random.uniform(ks[2], (HIDDEN, HIDDEN), jnp.float32, -scale, scale)
        w_v = jax.random.uniform(ks[3], (HIDDEN, HIDDEN), jnp.float32, -scale, scale)
        w_o = jax.random.uniform(ks[4], (HIDDEN, HIDDEN), jnp.float32, -scale, scale)
        return {'x': x, 'w_q': w_q, 'w_k': w_k, 'w_v': w_v, 'w_o': w_o}
    _L0_attn_in = _L0_attn_setup()

    def _L0_ffn_setup():
        import jax, jax.numpy as jnp
        import numpy as np
        import math
        SQRT7 = math.sqrt(7.0)
        EPS = 1e-05

        def int4_quant(x):
            beta = jnp.mean(jnp.abs(x), axis=-1, keepdims=True)
            x_q = jnp.clip(jnp.round(x * SQRT7 / (beta + EPS)), -8, 7)
            return x_q * (beta * SQRT7) / SQRT7

        def int8_quant(x):
            gamma = jnp.max(jnp.abs(x), axis=-1, keepdims=True)
            x_q = jnp.clip(jnp.round(x * 127.0 / (gamma + EPS)), -128, 127)
            return x_q * gamma / 127.0

        def bitlinear(x, w, scale):
            w_mean = jnp.mean(jnp.abs(w))
            w_q = jnp.clip(jnp.round(w / (w_mean + EPS)), -1.0, 1.0)
            w_eff = w_q * w_mean * scale
            return jnp.einsum('...i,oi->...o', x, w_eff)
        key = jax.random.key(seed)
        ks = jax.random.split(key, 4)
        H, I = (512, 1376)
        B, S = (2, 256)
        x = jax.random.normal(ks[0], (B, S, H), dtype=jnp.float32)
        w_gate = jax.random.uniform(ks[1], (I, H), jnp.float32, -1.0, 1.0) / np.sqrt(H)
        w_up = jax.random.uniform(ks[2], (I, H), jnp.float32, -1.0, 1.0) / np.sqrt(H)
        w_down = jax.random.uniform(ks[3], (H, I), jnp.float32, -1.0, 1.0) / np.sqrt(I)
        ones = jnp.ones((1,), jnp.float32)
        return {'x': x, 'w_gate': w_gate, 'w_up': w_up, 'w_down': w_down, 's_gate': ones, 's_up': ones, 's_down': ones}
    _L0_ffn_in = _L0_ffn_setup()
    _d = {'L0_attn_x': _L0_attn_in['x'], 'L0_attn_w_q': _L0_attn_in['w_q'], 'L0_attn_w_k': _L0_attn_in['w_k'], 'L0_attn_w_v': _L0_attn_in['w_v'], 'L0_attn_w_o': _L0_attn_in['w_o'], 'L0_ffn_w_gate': _L0_ffn_in['w_gate'], 'L0_ffn_w_up': _L0_ffn_in['w_up'], 'L0_ffn_w_down': _L0_ffn_in['w_down'], 'L0_ffn_s_gate': _L0_ffn_in['s_gate'], 'L0_ffn_s_up': _L0_ffn_in['s_up'], 'L0_ffn_s_down': _L0_ffn_in['s_down']}
    _x0 = _d['L0_attn_x']
    _d['L0_attn_x'] = jax.random.normal(jax.random.fold_in(jax.random.key(seed), 1), (2, 1024, 512), dtype=_x0.dtype)
    del _x0
    return _d

def reference(L0_attn_x, L0_attn_w_q, L0_attn_w_k, L0_attn_w_v, L0_attn_w_o, L0_ffn_w_gate, L0_ffn_w_up, L0_ffn_w_down, L0_ffn_s_gate, L0_ffn_s_up, L0_ffn_s_down):

    def _L0_attn_ref(x, w_q, w_k, w_v, w_o):
        import jax, jax.numpy as jnp
        import numpy as np
        HIDDEN = 512
        HEADS = 32
        D_K = HIDDEN // HEADS
        B, S, _ = x.shape

        def proj(w):
            y = jnp.einsum('bsd,ed->bse', x, w)
            return y.reshape(B, S, HEADS, D_K).transpose(0, 2, 1, 3)
        q, k, v = (proj(w_q), proj(w_k), proj(w_v))
        scores = jnp.einsum('bhqd,bhkd->bhqk', q, k) / jnp.sqrt(jnp.float32(D_K))
        attn = jax.nn.softmax(scores, axis=-1)
        out = jnp.einsum('bhqk,bhkd->bhqd', attn, v)
        out = out.transpose(0, 2, 1, 3).reshape(B, S, HIDDEN)
        return jnp.einsum('bse,oe->bso', out, w_o)

    def _L0_ffn_ref(x, w_gate, w_up, w_down, s_gate, s_up, s_down):
        import jax, jax.numpy as jnp
        import numpy as np
        import math
        SQRT7 = math.sqrt(7.0)
        EPS = 1e-05

        def int4_quant(x):
            beta = jnp.mean(jnp.abs(x), axis=-1, keepdims=True)
            x_q = jnp.clip(jnp.round(x * SQRT7 / (beta + EPS)), -8, 7)
            return x_q * (beta * SQRT7) / SQRT7

        def int8_quant(x):
            gamma = jnp.max(jnp.abs(x), axis=-1, keepdims=True)
            x_q = jnp.clip(jnp.round(x * 127.0 / (gamma + EPS)), -128, 127)
            return x_q * gamma / 127.0

        def bitlinear(x, w, scale):
            w_mean = jnp.mean(jnp.abs(w))
            w_q = jnp.clip(jnp.round(w / (w_mean + EPS)), -1.0, 1.0)
            w_eff = w_q * w_mean * scale
            return jnp.einsum('...i,oi->...o', x, w_eff)
        xq = int4_quant(x)
        gate = bitlinear(xq, w_gate, s_gate)
        up = bitlinear(xq, w_up, s_up)
        gate = jnp.square(jax.nn.relu(gate))
        inter = int8_quant(up * gate)
        return bitlinear(inter, w_down, s_down)
    x = L0_attn_x
    x = x + _L0_attn_ref(_layernorm(x, axis=-1), L0_attn_w_q, L0_attn_w_k, L0_attn_w_v, L0_attn_w_o)
    x = x + _L0_ffn_ref(_layernorm(x, axis=-1), L0_ffn_w_gate, L0_ffn_w_up, L0_ffn_w_down, L0_ffn_s_gate, L0_ffn_s_up, L0_ffn_s_down)
    return x

_drawn_inputs = setup_inputs


def setup_inputs(seed=0):
    import zlib

    import numpy as np

    out = dict(_drawn_inputs(seed))
    spreads = {}
    factors = {}
    for name, (base, spread) in spreads.items():
        noise = np.random.default_rng([zlib.crc32(name.encode()), seed]).standard_normal(out[name].shape)
        drawn = base * np.exp(spread * noise) if base else spread * noise
        out[name] = jnp.asarray(drawn.astype(out[name].dtype))
    for name, factor in factors.items():
        out[name] = (out[name] * factor).astype(out[name].dtype)
    return out
```

```python
from contextlib import ExitStack

import numpy as np

import concourse.bass as bass
from concourse import mybir

ALU = mybir.AluOpType
ACT = mybir.ActivationFunctionType
AX = mybir.AxisListType
F32 = mybir.dt.float32
BF16 = mybir.dt.bfloat16

P = 128
BATCH, SEQ, HID = 2, 1024, 512
HEADS, DK = 32, 16
INTER = 1376
LN_EPS = 1e-5
Q_EPS = 1e-5
SQRT7 = float(np.sqrt(7.0))
MAGIC = 12582912.0

TOK = BATCH * SEQ
TILES = TOK // P
KT = HID // P
SH = P // DK
SUPERS = BATCH * HEADS // SH
SPB = HEADS // SH
GH = 4
HALF = 512
KEYT = SEQ // P
STEPS = 4 * KEYT
AHEAD = 11
ROWS = 6 * DK
AUG = ROWS + 3
IT = (INTER + P - 1) // P
ILAST = INTER - (IT - 1) * P
CH = INTER // 4
WCOL = KT * INTER
DCOL = IT * HID


def build(nc, x, wqT, wkT, wvT, woT, wgT, wuT, wdT, s_gate, s_up, s_down, out):
    ctx = ExitStack()
    with ctx:
        def sb(name, shape, dt):
            return ctx.enter_context(nc.sbuf_tensor(name, shape, dt))

        def sem(name):
            return ctx.enter_context(nc.semaphore(name))

        parts_d = nc.dram_tensor("parts_d", [SUPERS, 2, 3 * DK, SH, SEQ], BF16, kind="Internal").ap()
        att_d = nc.dram_tensor("att_d", [BATCH, 2 * DK, SH, SPB, SEQ], F32, kind="Internal").ap()
        rden_d = nc.dram_tensor("rden_d", [BATCH, SH, SPB, SEQ], F32, kind="Internal").ap()

        XV = sb("XV", [P, 4, 4096], F32)
        QK = sb("QK", [P, 2, 2, GH, SEQ], BF16)
        PB = sb("PB", [P, 2, GH, HALF], F32)
        spl = sb("spl", [P, 2, 3, HALF], BF16)
        qk32 = sb("qk32", [P, 2, HALF], F32)
        Vg = sb("Vg", [P, 2, KEYT, GH, 32], F32)
        wqk = sb("wqk", [P, 2, KT, P], F32)
        wv = sb("wv", [P, KT, HID], F32)
        wo = sb("wo", [P, KT, HID], F32)
        OS = sb("OS", [P, 2, HALF], F32)
        tg = sb("tg", [P, KT, INTER], BF16)
        tu = sb("tu", [P, KT, INTER], BF16)
        td = sb("td", [P, IT, HID], BF16)
        ident = sb("ident", [P, P], F32)
        identb = sb("identb", [P, P], BF16)
        ones = sb("ones", [P, P], F32)
        expo = sb("expo", [P, 4], F32)
        bst = sb("bst", [P, 4, 6], F32)
        bag = sb("bag", [P, 4, 2], F32)
        vpe = sb("vpe", [P, 4], F32)
        rstd = sb("rstd", [P, 4], F32)
        mx = sb("mx", [P, 2, 16, 2], F32)
        nm = sb("nm", [P, 2, 16], F32)
        nmr = sb("nmr", [P, 2, 16], F32)
        nmb = sb("nmb", [P, 4, 3, GH], BF16)
        nmT = sb("nmT", [3 * GH, 2, HALF], BF16)
        wsum = sb("wsum", [P, 3, 4], F32)
        wtot = sb("wtot", [P, 3], F32)
        wmean = sb("wmean", [P, 3], F32)
        wrec = sb("wrec", [P, 3], F32)
        wfac = sb("wfac", [P, 3], F32)
        srow = sb("srow", [1, 3], F32)

        scal = sb("scal", [P, 3], F32)
        wfd = sb("wfd", [P, 1], F32)
        magic = sb("magic", [P, 1], F32)
        bsum = sb("bsum", [P, 2], F32)
        bq = sb("bq", [P, 2, 3], F32)
        agu = sb("agu", [P, 2, 2], F32)
        hm = sb("hm", [P, 2, 8], F32)

        xin = PB[:, 0]
        xnr = PB[:, 1]
        stg = OS[:, :, :].rearrange("p s (k t) -> p s k t", k=KT)
        raw_g = QK[:, :, :, :, :].rearrange("p s q h t -> p (s q h t)").bitcast(F32)[:, 0:WCOL]
        raw_u = XV[:, 1:3, :].rearrange("p a n -> p (a n)")[:, 0:WCOL]
        tern = [tg[:, :, :].rearrange("p k n -> p (k n)"), tu[:, :, :].rearrange("p k n -> p (k n)"),
                td[:, :, :].rearrange("p k n -> p (k n)")]
        DQ = DCOL // 4

        def raw(w, q):
            if w < 2:
                n = WCOL // 4
                return (raw_g, raw_u)[w][:, q * n:(q + 1) * n]
            return XV[:, (0, 3)[q // 2], (q % 2) * DQ:(q % 2 + 1) * DQ]

        def ternq(w, q):
            n = (WCOL, WCOL, DCOL)[w] // 4
            return tern[w][:, q * n:(q + 1) * n]

        num = [XV[:, 1, :].rearrange("p (g t) -> p g t", g=SPB), XV[:, 2, :].rearrange("p (g t) -> p g t", g=SPB)]
        rdn = QK[:, :, :, :, :].rearrange("p s q h t -> p (s q h t)").bitcast(F32).rearrange(
            "p (b g t) -> p b g t", b=BATCH, g=SPB)
        den = qk32[:, :, 0:256]
        xh = XV[:, 0, 0:1024].rearrange("p (s n) -> p s n", s=2)
        att = XV[:, 0, 1024:2048].rearrange("p (s g t) -> p s g t", s=2, g=SPB)
        junk = XV[:, 0, 2048:2560]
        hin = XV[:, 3, 0:2 * INTER].rearrange("p (s n) -> p s n", s=2)
        rel = XV[:, 3, 2 * INTER:2 * INTER + 2 * CH].rearrange("p (s n) -> p s n", s=2)
        xr = PB[:, 0]
        outt = PB[:, 1, 0:2]
        vgb = Vg[:, :, :, :, :].rearrange("p s k h d -> p (s k h d)").bitcast(BF16)
        xq = vgb[:, 0:1024].rearrange("p (s n) -> p s n", s=2)
        xqT = vgb[:, 1024:2048].rearrange("p (s k t) -> p s k t", s=2, k=KT)
        qi = spl[:, :, :, :].rearrange("p s a n -> p (s a n)")[:, 0:2 * INTER].rearrange("p (s n) -> p s n", s=2)
        qiT = wv[:, :, :].rearrange("p k n -> p (k n)").bitcast(BF16)[:, 0:2 * IT * P].rearrange(
            "p (s k t) -> p s k t", s=2, k=IT)

        def xT(region, kt, start, n):
            if isinstance(region, int):
                return XV[:, region, kt * SEQ + start:kt * SEQ + start + n]
            return XV[:, 0:2, :].rearrange("p r n -> p (r n)")[:, bass.ds(region * 4096 + (kt * SEQ + start), n)]

        ps = ctx.enter_context(nc.psum_tensor("ps", [P, 8, 512], F32))

        x_in = [sem(f"x_in{r}") for r in range(4)]
        s_in, wv_in, wo_in, wq_in, wk_in = sem("s_in"), sem("wv_in"), sem("wo_in"), sem("wq_in"), sem("wk_in")
        raw_in = [sem(f"raw_in{w}") for w in range(3)]
        consts, ident_ok = sem("consts"), sem("ident_ok")
        bn_step, stats, var_ok, rs_ready = sem("bn_step"), sem("stats"), sem("var_ok"), sem("rs_ready")
        xn_ready, xt_psum, xt_stg, xt_copy = sem("xn_ready"), sem("xt_psum"), sem("xt_stg"), sem("xt_copy")
        v_psum, v_copy = sem("v_psum"), sem("v_copy")
        w_abs, w_tot, w_psum, w_fac, w_step = sem("w_abs"), sem("w_tot"), sem("w_psum"), sem("w_fac"), sem("w_step")
        w_round, w_min, w_tern, s_psum3 = sem("w_round"), sem("w_min"), sem("w_tern"), sem("s_psum3")
        job_psum, job_copy, job_split, spl_step = sem("job_psum"), sem("job_copy"), sem("job_split"), sem("spl_step")
        parts_out = [sem(f"parts_out{r}") for r in range(2)]
        stack_in = [sem(f"stack_in{s}") for s in range(2)]
        ones_set, vg_ready = sem("ones_set"), sem("vg_ready")
        s_psum, s_used = sem("s_psum"), sem("s_used")
        nm_ready, nm_step, nm_parts = sem("nm_ready"), sem("nm_step"), sem("nm_parts")
        nm_in = [sem(f"nm_in{r}") for r in range(2)]
        st_psum, probs, av_done = sem("st_psum"), sem("probs"), sem("av_done")
        os_copy, os_out = sem("os_copy"), [sem(f"os_out{r}") for r in range(2)]
        den_in = [sem(f"den_in{b}") for b in range(2)]
        num_in = [sem(f"num_in{b}") for b in range(2)]
        rdn_in = [sem(f"rdn_in{b}") for b in range(2)]
        den_rec, rden_out = sem("den_rec"), sem("rden_out")
        xr_in = [sem(f"xr_in{r}") for r in range(4)]
        att_ready, o_psum, x2_ready, f_stats = sem("att_ready"), sem("o_psum"), sem("x2_ready"), sem("f_stats")
        f_bn, f_var, f_rs, xh_ready, x_abs = sem("f_bn"), sem("f_var"), sem("f_rs"), sem("xh_ready"), sem("x_abs")
        q_step, xq_ready, xq_psum, xq_copy = sem("q_step"), sem("xq_ready"), sem("xq_psum"), sem("xq_copy")
        g_psum, u_psum, rel_ready, sq_ready = sem("g_psum"), sem("u_psum"), sem("rel_ready"), sem("sq_ready")
        h_ready, hm_step, hs_ready, y_ready, qi_ready = (sem("h_ready"), sem("hm_step"), sem("hs_ready"),
                                                         sem("y_ready"), sem("qi_ready"))
        qt_psum, qt_copy, d_psum, o_ready = sem("qt_psum"), sem("qt_copy"), sem("d_psum"), sem("o_ready")
        out_done = [sem(f"out_done{r}") for r in range(4)]
        scal_ok, down_zero, waits_carried = sem("scal_ok"), sem("down_zero"), sem("waits_carried")
        block = ctx.enter_context(nc.Block())

        def own_wait(eng, semaphore, value):
            eng.wait_ge(semaphore, value)
            eng.sem_inc(waits_carried, 1)

        def first(n, limit):
            return isinstance(n, int) and n < limit

        def item_at(sup, unit, k):
            rest = 33 * unit + k - (1 if k < 8 and not (first(sup, 1) and unit == 0) else 0)
            return rest

        def rows_at(sup, unit):
            return 33 * unit + (40 if not (isinstance(sup, int) and sup == SUPERS - 1 and unit == 3) else 32)

        def step_items(step):
            found = []
            for j in range(4):
                n = (step + AHEAD) * 4 + j
                found.append((n // 128, n % 128 // 32, n % 32))
            return found

        def rows_unit(step):
            if step % KEYT != 6:
                return None
            u = step // KEYT + 1
            return (u // 4, u % 4)

        def pe_tile_transpose(pe, j, r):
            t = j * 4 + r
            pe.wait_ge(xn_ready, t + 1)
            if not first(t, 2):
                pe.wait_ge(xt_stg, t - 1)
            for k in range(KT):
                last = nc.tensor.transpose(ps[:, r % 2, k * P:(k + 1) * P], xnr[:, r, k * P:(k + 1) * P], ident[:])
            last.then_inc(xt_psum, 1)

        def pe_tile_values(pe, j, r):
            t = j * 4 + r
            pe.wait_ge(xt_stg, t + 1)
            if not first(t, 2):
                pe.wait_ge(v_copy, t - 1)
            for k in range(KT):
                last = nc.tensor.matmul(ps[:, 2 + r % 2, :], stg[:, r % 2, k, :], wv[:, k, :],
                                        start=(k == 0), stop=(k == KT - 1))
            last.then_inc(v_psum, 1)

        def pe_tiles(pe, j):
            pe_tile_transpose(pe, j, 0)
            for r in range(4):
                if r < 3:
                    pe_tile_transpose(pe, j, r + 1)
                pe_tile_values(pe, j, r)

        def pe_mean(pe, w):
            pe.wait_ge(w_tot, w + 1)
            nc.tensor.matmul(ps[:, 7, 8 * w:8 * w + 1], ones[:], wtot[:, w:w + 1], start=True, stop=True)\
                .then_inc(w_psum, 1)

        def pe_job(pe, sup, region, job, k):
            qk, half = job // 2, job % 2
            n = sup * 4 + job
            if k == 0:
                if half == 0:
                    pe.wait_ge((wq_in, wk_in)[qk], sup * 16 + 16)
                if not first(n, 1):
                    pe.wait_ge(job_copy, n)
            last = nc.tensor.matmul(ps[:, 7, :], wqk[:, qk, k, :], xT(region, k, half * HALF, HALF),
                                    start=(k == 0), stop=(k == KT - 1))
            if k == KT - 1:
                last.then_inc(job_psum, 1)

        def pe_scores(pe, sup, unit, k):
            slot, j = k // 4, k % 4
            qt, head, kh = slot // 2, (slot % 2) * 2 + j // 2, j % 2
            set_, half = unit // 2, unit % 2
            at = item_at(sup, unit, k)
            if k == 0 and half == 0:
                pe.wait_ge(stack_in[set_], sup * 96 + 96)
            if not (isinstance(sup, int) and sup * 132 + at < 2):
                pe.wait_ge(s_used, sup * 132 + (at - 1))
            nc.tensor.matmul(ps[:, 4 + at % 2, :],
                             QK[0:ROWS, set_, 0, head, half * HALF + qt * P:half * HALF + (qt + 1) * P],
                             QK[0:ROWS, set_, 1, head, kh * HALF:(kh + 1) * HALF],
                             start=True, stop=True).then_inc(s_psum, 1)

        def pe_max_rows(pe, sup, unit):
            at = rows_at(sup, unit)
            pe.wait_ge(nm_parts, sup * 4 + (unit + 1))
            pe.wait_ge(s_used, sup * 132 + (at - 1))
            dst = ps[0:3 * GH, 4 + at % 2, :].bitcast(BF16)
            for qt in range(4):
                last = nc.tensor.transpose(dst[:, qt * P:(qt + 1) * P],
                                           nmb[:, qt, :, :].rearrange("p a h -> p (a h)"), identb[:])
            last.then_inc(s_psum, 1)

        def pe_scoresT(pe, sup, step, pair):
            unit, kt = step // KEYT, step % KEYT
            set_, half = unit // 2, unit % 2
            if kt == 0 and pair == 0:
                pe.wait_ge(nm_in[half], sup * 32 + 16 * (set_ + 2))
            if step > 0:
                pe.wait_ge(probs, sup * (2 * STEPS) + (2 * step + pair - 1))
            for h2 in range(2):
                head = pair * 2 + h2
                last = nc.tensor.matmul(ps[:, 2 * pair + h2, :], QK[0:AUG, set_, 1, head, kt * P:(kt + 1) * P],
                                        QK[0:AUG, set_, 0, head, half * HALF:(half + 1) * HALF],
                                        start=True, stop=True)
            last.then_inc(st_psum, 1)

        def pe_av(pe, sup, step):
            unit, kt = step // KEYT, step % KEYT
            set_ = unit // 2
            pe.wait_ge(probs, sup * (2 * STEPS) + (2 * step + 2))
            if kt == 0:
                if unit % 2 == 0:
                    pe.wait_ge(vg_ready, sup * 2 + (set_ + 1))
                pe.wait_ge(os_copy, sup * 4 + (unit + 1))
            for h in range(GH):
                last = nc.tensor.matmul(ps[32 * h:32 * h + 32, 6, :], Vg[:, set_, kt, h, :], PB[:, step % 2, h, :],
                                        start=(kt == 0), stop=(kt == KEYT - 1))
            last.then_inc(av_done, 1)

        def pe_superunit(pe, sup, region, last):
            for step in range(STEPS):
                items = [(lambda a=a, u=u, k=k: pe_scores(pe, sup + a, u, k)) if not (last and a) else (lambda: None)
                         for a, u, k in step_items(step)]
                items[0]()
                pe_scoresT(pe, sup, step, 0)
                items[1]()
                pe_scoresT(pe, sup, step, 1)
                if not last and step < 16:
                    pe_job(pe, sup + 1, region, step // 4, step % 4)
                items[2]()
                if step > 0:
                    pe_av(pe, sup, step - 1)
                items[3]()
                rows = rows_unit(step)
                if rows and not (last and rows[0]):
                    pe_max_rows(pe, sup + rows[0], rows[1])
                if last and step == 20:
                    pe_mean(pe, 2)
            pe_av(pe, sup, STEPS - 1)

        def pe_attention_out(pe, t, r):
            pe.wait_ge(att_ready, t + 1)
            if not first(t, 1):
                pe.wait_ge(x2_ready, t)
            for g in range(SPB):
                last = nc.tensor.matmul(ps[:, 0, :], att[:, r % 2, g, :], wo[:, g, :],
                                        start=(g == 0), stop=(g == SPB - 1))
            last.then_inc(o_psum, 1)

        def pe_xq_transpose(pe, t, r):
            pe.wait_ge(xq_ready, t + 1)
            if not first(t, 2):
                pe.wait_ge(qt_copy, (t - 1) * 2)
            dst = ps[:, 1, :].bitcast(BF16)
            for k in range(KT):
                last = nc.tensor.transpose(dst[:, k * P:(k + 1) * P], xq[:, r % 2, k * P:(k + 1) * P], identb[:])
            last.then_inc(xq_psum, 1)

        def pe_gate_up(pe, t, r):
            pe.wait_ge(xq_copy, t + 1)
            for c in range(4):
                n = t * 4 + c
                for w, bank, ready, used in ((tg, 2, g_psum, rel_ready), (tu, 4, u_psum, h_ready)):
                    if not first(n, 2):
                        pe.wait_ge(used, n - 1)
                    for k in range(KT):
                        last = nc.tensor.matmul(ps[:, bank + c % 2, 0:CH], xqT[:, r % 2, k, :],
                                                w[:, k, c * CH:(c + 1) * CH], start=(k == 0), stop=(k == KT - 1))
                    last.then_inc(ready, 1)

        def pe_inner_transpose(pe, t, r):
            pe.wait_ge(qi_ready, t + 1)
            if not first(t, 1):
                pe.wait_ge(qt_copy, t * 2)
            for k in range(IT):
                n = P if k < IT - 1 else ILAST
                dst = ps[:, 6, :].bitcast(BF16)[0:n, k * P:(k + 1) * P] if k < 8 else \
                    ps[:, 1, :].bitcast(BF16)[0:n, (k - 4) * P:(k - 3) * P]
                last = nc.tensor.transpose(dst, qi[:, r % 2, k * P:k * P + n], identb[:])
                if k in (7, IT - 1):
                    last.then_inc(qt_psum, 1)

        def pe_down(pe, t, r):
            pe.wait_ge(qt_copy, t * 2 + 2)
            if not first(t, 1):
                pe.wait_ge(o_ready, t)
            for k in range(IT):
                n = P if k < IT - 1 else ILAST
                last = nc.tensor.matmul(ps[:, 7, :], qiT[0:n, r % 2, k, :], td[0:n, k, :],
                                        start=(k == 0), stop=(k == IT - 1))
            last.then_inc(d_psum, 1)

        def positions(run, eng, one):
            def at(p, r):
                def tile(delta):
                    t = p + delta
                    return (t, (r + delta) % 4) if not isinstance(t, int) or 0 <= t < TILES else None
                one(tile)
            for p in (-2, -1, 0, 1):
                at(p, p % 4)
            with eng.Fori(0, 3) as m:
                for r in range(4):
                    at(m * 4 + (2 + r), (2 + r) % 4)
            for p in (14, 15, 16):
                at(p, p % 4)

        def stage(tile, delta, do, *more):
            found = tile(delta)
            if found:
                do(*found)

        @block.tensor
        def _(pe):
            pe.wait_ge(consts, 8)
            pe.wait_ge(ident_ok, 2)
            pe.wait_ge(wv_in, 16)
            for j in range(2):
                pe_tiles(pe, j)
            pe.wait_ge(xt_copy, 8)
            for job in range(4):
                for k in range(KT):
                    pe_job(pe, 0, 0, job, k)
            pe.wait_ge(job_copy, 4)
            pe.wait_ge(s_in, 48)
            nc.tensor.matmul(ps[:, 7, 32:35], ones[0:1, :], srow[:], start=True, stop=True).then_inc(s_psum3, 1)
            pe_mean(pe, 0)
            pe_mean(pe, 1)
            with pe.Fori(2, 4) as j:
                pe_tiles(pe, j)
            for k in range(4 * AHEAD):
                pe_scores(pe, 0, k // 32, k % 32)
                if k == 39:
                    pe_max_rows(pe, 0, 0)
            pe.wait_ge(w_fac, 2)
            pe.wait_ge(xt_copy, TILES)
            pe.wait_ge(v_copy, TILES)
            with pe.Fori(0, SUPERS - 1) as i:
                pe_superunit(pe, i, (i + 1) // SPB, False)
            pe_superunit(pe, SUPERS - 1, 1, True)
            pe.wait_ge(os_copy, 4 * SUPERS + 1)
            pe.wait_ge(s_used, 132 * SUPERS)
            pe.wait_ge(wo_in, 64)
            pe.wait_ge(w_tern, 12)
            pe.wait_ge(w_fac, 3)

            def one(tile):
                stage(tile, 0, lambda t, r: pe_gate_up(pe, t, r))
                stage(tile, -1, lambda t, r: pe_inner_transpose(pe, t, r))
                stage(tile, 2, lambda t, r: pe_attention_out(pe, t, r))
                stage(tile, -1, lambda t, r: pe_down(pe, t, r))
                stage(tile, 1, lambda t, r: pe_xq_transpose(pe, t, r))
            positions(None, pe, one)

        def act_tiles(act, j):
            for r in range(4):
                t = j * 4 + r
                act.wait_ge(xt_psum, t + 1)
                if not first(t, 2):
                    act.wait_ge(v_psum, t - 1)
                    act.wait_ge(xt_copy, t - 1)
                nc.scalar.activation(stg[:, r % 2].rearrange("p k t -> p (k t)"), ps[:, r % 2, :], ACT.Copy)\
                    .then_inc(xt_stg, 1)
                act.wait_ge(v_psum, t + 1)
                if isinstance(j, int):
                    dst = XV[:, 3, t * HID:(t + 1) * HID]
                else:
                    dst = XV[:, 2, bass.ds((j - 2) * (4 * HID) + r * HID, HID)]
                nc.scalar.activation(dst, ps[:, 2 + r % 2, :], ACT.Copy).then_inc(v_copy, 1)

        def act_job(act, sup, job):
            n = sup * 4 + job
            act.wait_ge(job_psum, n + 1)
            if not first(n, 2):
                act.wait_ge(job_split, n - 1)
            nc.scalar.activation(qk32[:, job % 2, :], ps[:, 7, :], ACT.Copy).then_inc(job_copy, 1)

        def act_abs(act, w, q):
            if q == 0:
                act.wait_ge(raw_in[w], 16 * (1, 1, 5)[w])
                if w == 2:
                    act.wait_ge(down_zero, 1)
            nc.scalar.activation(ternq(w, q), raw(w, q), ACT.Abs, accum_out=wsum[:, w, q:q + 1]).then_inc(w_abs, 1)

        def act_round(act, w, q):
            if q == 0:
                act.wait_ge(w_fac, w + 1)
            act.wait_ge(w_abs, 4 * w + q + 1)
            nc.scalar.activation(raw(w, q), raw(w, q), ACT.Identity, bias=magic[:], scale=wrec[:, w:w + 1])\
                .then_inc(w_round, 1)

        def act_exp(act, sup, step, pair):
            n = 2 * step + pair
            act.wait_ge(st_psum, sup * (2 * STEPS) + (n + 1))
            if pair == 0 and step > 1:
                act.wait_ge(av_done, sup * STEPS + (step - 1))
            nc.scalar.activation(PB[:, step % 2, 2 * pair:2 * pair + 2, :], ps[:, 2 * pair:2 * pair + 2, :],
                                 ACT.Exp, scale=1.0 / float(np.sqrt(DK))).then_inc(probs, 1)

        def act_sums(act, sup, unit):
            act.wait_ge(av_done, sup * STEPS + KEYT * (unit + 1))
            act.wait_ge(os_out[unit % 2], sup * 32 + 16 * (unit // 2 + 1))
            nc.scalar.activation(OS[:, unit % 2, :], ps[:, 6, :], ACT.Copy).then_inc(os_copy, 1)

        def act_superunit(act, sup, last):
            for step in range(STEPS):
                act_exp(act, sup, step, 0)
                act_exp(act, sup, step, 1)
                if step % KEYT == 0 and step > 0:
                    act_sums(act, sup, step // KEYT - 1)
                if not last and step < 16 and step % 4 == 3:
                    act_job(act, sup + 1, step // 4)
                if last and step in (12, 14, 16, 18):
                    act_abs(act, 2, (step - 12) // 2)
                if last and step in (23, 25, 27, 29):
                    act_round(act, 2, (step - 23) // 2)
            act_sums(act, sup, 3)

        def act_abs_x(act, t, r):
            act.wait_ge(xh_ready, t + 1)
            if not first(t, 2):
                act.wait_ge(xq_ready, t - 1)
            if not first(t, 1):
                act.wait_ge(x_abs, t)
            nc.scalar.activation(junk, xh[:, r % 2, :], ACT.Abs, accum_out=bsum[:, r % 2:r % 2 + 1]).then_inc(x_abs, 1)

        def act_xq_copy(act, t, r):
            act.wait_ge(xq_psum, t + 1)
            if not first(t, 2):
                act.wait_ge(u_psum, (t - 1) * 4)
            nc.scalar.activation(xqT[:, r % 2].rearrange("p k t -> p (k t)"), ps[:, 1, :].bitcast(BF16)[:, 0:HID],
                                 ACT.Copy).then_inc(xq_copy, 1)

        def act_gate(act, t, r):
            for c in range(4):
                n = t * 4 + c
                act.wait_ge(g_psum, n + 1)
                if not first(n, 2):
                    act.wait_ge(h_ready, n - 1)
                nc.scalar.activation(rel[:, c % 2, :], ps[:, 2 + c % 2, 0:CH], ACT.Relu,
                                     scale=agu[:, r % 2, 0:1]).then_inc(rel_ready, 1)
                act.wait_ge(rel_ready, n + 1)
                nc.scalar.activation(rel[:, c % 2, :], rel[:, c % 2, :], ACT.Square).then_inc(sq_ready, 1)

        def act_inner_round(act, t, r):
            act.wait_ge(hs_ready, t + 1)
            nc.scalar.activation(hin[:, r % 2, :], hin[:, r % 2, :], ACT.Identity, bias=magic[:],
                                 scale=hm[:, r % 2, 5:6]).then_inc(y_ready, 1)

        def act_inner_copy(act, t, r):
            act.wait_ge(qt_psum, t * 2 + 1)
            if not first(t, 1):
                act.wait_ge(d_psum, t)
            nc.scalar.activation(qiT[:, r % 2, 0:8, :].rearrange("p k t -> p (k t)"), ps[:, 6, :].bitcast(BF16),
                                 ACT.Copy).then_inc(qt_copy, 1)
            act.wait_ge(qt_psum, t * 2 + 2)
            src = ps[:, 1, :].bitcast(BF16)
            nc.scalar.activation(qiT[:, r % 2, 8:10, :].rearrange("p k t -> p (k t)"), src[:, 4 * P:6 * P], ACT.Copy)
            nc.scalar.activation(qiT[0:ILAST, r % 2, 10, :], src[0:ILAST, 6 * P:7 * P], ACT.Copy).then_inc(qt_copy, 1)

        @block.scalar
        def _(act):
            act.wait_ge(consts, 8)
            for j in range(2):
                act_tiles(act, j)
            for job in range(4):
                act_job(act, 0, job)
            for w in range(2):
                for q in range(4):
                    act_abs(act, w, q)
            for w in (1, 0):
                for q in range(4):
                    act_round(act, w, q)
            act.wait_ge(w_min, 8)
            with act.Fori(2, 4) as j:
                act_tiles(act, j)
            with act.Fori(0, SUPERS - 1) as i:
                act_superunit(act, i, False)
            act_superunit(act, SUPERS - 1, True)
            act.wait_ge(w_tern, 12)

            def one(tile):
                stage(tile, 0, lambda t, r: act_gate(act, t, r))
                stage(tile, -1, lambda t, r: act_inner_copy(act, t, r))
                stage(tile, 1, lambda t, r: act_abs_x(act, t, r))
                stage(tile, 0, lambda t, r: act_inner_round(act, t, r))
                stage(tile, 1, lambda t, r: act_xq_copy(act, t, r))
            positions(None, act, one)

        def dve_tiles(dve, j):
            for r in range(4):
                t = j * 4 + r
                dve.wait_ge(x_in[r], j * 16 + 16)
                if not first(j, 1):
                    dve.wait_ge(stats, j)
                nc.vector.bn_stats(bst[:, r, :], xin[:, r, :]).then_inc(bn_step, 1)
            own_wait(dve, bn_step, j * 4 + 4)
            for r in range(4):
                last = nc.vector.bn_aggr(bag[:, r, :], bst[:, r, :])
            last.then_inc(stats, 1)
            dve.wait_ge(stats, j + 1)
            dve.wait_ge(rs_ready, j + 1)
            for r in range(4):
                t = j * 4 + r
                if not first(j, 1):
                    dve.wait_ge(xt_psum, t - 3)
                nc.vector.tensor_scalar(xnr[:, r, :], xin[:, r, :], bag[:, r, 0:1], rstd[:, r:r + 1],
                                        ALU.subtract, ALU.mult).then_inc(xn_ready, 1)
            for r in range(4):
                t = j * 4 + r
                dve.wait_ge(xt_stg, t + 1)
                if isinstance(j, int):
                    region = XV[:, 0, :].rearrange("p (k t) -> p k t", k=KT)
                    dst = region[:, :, t * P:(t + 1) * P]
                else:
                    region = XV[:, 1, :].rearrange("p (k t) -> p k t", k=KT)
                    dst = region[:, :, bass.ds((j - 2) * (4 * P) + r * P, P)]
                nc.vector.tensor_copy(dst, stg[:, r % 2]).then_inc(xt_copy, 1)

        def dve_total(dve, w):
            dve.wait_ge(w_abs, 4 * w + 4)
            nc.vector.reduce_sum(wtot[:, w:w + 1], wsum[:, w, :], AX.X).then_inc(w_tot, 1)

        def dve_factor(dve, w):
            dve.wait_ge(w_psum, w + 1)
            nc.vector.tensor_scalar(wmean[:, w:w + 1], ps[:, 7, 8 * w:8 * w + 1], 1.0 / (INTER * HID), None, ALU.mult)\
                .then_inc(w_step, 1)
            dve.wait_ge(w_step, 3 * w + 1)
            nc.vector.tensor_scalar(wrec[:, w:w + 1], wmean[:, w:w + 1], Q_EPS, None, ALU.add).then_inc(w_step, 1)
            nc.vector.tensor_tensor(wfac[:, w:w + 1], scal[:, w:w + 1], wmean[:, w:w + 1], ALU.mult)\
                .then_inc(w_step, 1)
            dve.wait_ge(w_step, 3 * w + 3)
            nc.vector.reciprocal(wrec[:, w:w + 1], wrec[:, w:w + 1]).then_inc(w_fac, 1)

        def dve_ternary(dve, w, q, order):
            dve.wait_ge(w_round, order + 1)
            nc.vector.tensor_scalar(ternq(w, q), raw(w, q), MAGIC, 1.0, ALU.subtract, ALU.min).then_inc(w_min, 1)
            dve.wait_ge(w_min, order + 1)
            nc.vector.tensor_scalar(ternq(w, q), ternq(w, q), -1.0, None, ALU.max).then_inc(w_tern, 1)

        def dve_max(dve, sup, unit, k):
            slot, j = k // 4, k % 4
            qt, head, kh = slot // 2, (slot % 2) * 2 + j // 2, j % 2
            at = item_at(sup, unit, k)
            dve.wait_ge(s_psum, sup * 132 + (at + 1))
            if k == 0 and not (isinstance(sup, int) and sup * 4 + unit < 2):
                dve.wait_ge(nm_ready, sup * 4 + (unit - 1))
            nc.vector.tensor_reduce(mx[:, unit % 2, qt * 4 + head, kh:kh + 1], ps[:, 4 + at % 2, :], AX.X, ALU.max)\
                .then_inc(s_used, 1)
            if k == 31:
                dve.wait_ge(s_used, sup * 132 + (at + 1))
                if not (isinstance(sup, int) and sup * 4 + unit < 1):
                    dve.wait_ge(nm_parts, sup * 4 + unit)
                nc.vector.tensor_reduce(nm[:, unit % 2, :], mx[:, unit % 2, :, :], AX.X, ALU.max, negate=True)\
                    .then_inc(nm_ready, 1)

        def dve_rows(dve, sup, unit):
            at = rows_at(sup, unit)
            dve.wait_ge(s_psum, sup * 132 + (at + 1))
            dve.wait_ge(nm_in[unit % 2], sup * 32 + 16 * (unit // 2 + 1))
            nc.vector.tensor_copy(nmT[:, unit % 2, :], ps[0:3 * GH, 4 + at % 2, :].bitcast(BF16)[:, 0:HALF])\
                .then_inc(s_used, 1)

        def dve_superunit(dve, sup, last):
            for step in range(STEPS):
                for a, u, k in step_items(step):
                    if not (last and a):
                        dve_max(dve, sup + a, u, k)
                rows = rows_unit(step)
                if rows and not (last and rows[0]):
                    dve_rows(dve, sup + rows[0], rows[1])
                if last and step == 20:
                    dve_total(dve, 2)
                    dve_factor(dve, 2)

        def dve_reciprocal(dve, b):
            dve.wait_ge(den_in[b], 16)
            nc.vector.reciprocal(den[:, b, :], den[:, b, :]).then_inc(den_rec, 1)

        def dve_x2(dve, t, r):
            dve.wait_ge(o_psum, t + 1)
            dve.wait_ge(xr_in[r], xr_count(t, r))
            nc.vector.tensor_tensor(xr[:, r, :], ps[:, 0, :], xr[:, r, :], ALU.add).then_inc(x2_ready, 1)
            dve.wait_ge(x2_ready, t + 1)
            nc.vector.bn_stats(bst[:, r, :], xr[:, r, :]).then_inc(f_bn, 1)
            own_wait(dve, f_bn, t + 1)
            nc.vector.bn_aggr(bag[:, r, :], bst[:, r, :]).then_inc(f_stats, 1)

        def dve_xh(dve, t, r):
            dve.wait_ge(f_rs, t + 1)
            if not first(t, 2):
                dve.wait_ge(xq_ready, t - 1)
            nc.vector.tensor_scalar(xh[:, r % 2, :], xr[:, r, :], bag[:, r, 0:1], rstd[:, r:r + 1],
                                    ALU.subtract, ALU.mult).then_inc(xh_ready, 1)

        def dve_quant(dve, t, r):
            s = r % 2
            n = 5 * t
            dve.wait_ge(x_abs, t + 1)
            nc.vector.tensor_scalar(bq[:, s, 0:1], bsum[:, s:s + 1], 1.0 / HID, Q_EPS, ALU.mult, ALU.add)\
                .then_inc(q_step, 1)
            if not first(t, 2):
                dve.wait_ge(hs_ready, t - 1)
            nc.vector.tensor_scalar(agu[:, s, :], wfac[:, 0:2], bsum[:, s:s + 1], 1.0 / HID, ALU.mult, ALU.mult)
            dve.wait_ge(q_step, n + 1)
            nc.vector.reciprocal(bq[:, s, 1:2], bq[:, s, 0:1]).then_inc(q_step, 1)
            dve.wait_ge(q_step, n + 2)
            nc.vector.tensor_scalar(bq[:, s, 2:3], bq[:, s, 1:2], SQRT7, None, ALU.mult).then_inc(q_step, 1)
            dve.wait_ge(q_step, n + 3)
            nc.vector.tensor_scalar(xh[:, s, :], xh[:, s, :], bq[:, s, 2:3], 7.0, ALU.mult, ALU.min).then_inc(q_step, 1)
            dve.wait_ge(q_step, n + 4)
            nc.vector.tensor_scalar(xh[:, s, :], xh[:, s, :], -8.0, MAGIC, ALU.max, ALU.add).then_inc(q_step, 1)
            dve.wait_ge(q_step, n + 5)
            if not first(t, 2):
                dve.wait_ge(xq_psum, t - 1)
            nc.vector.tensor_scalar(xq[:, s, :], xh[:, s, :], MAGIC, None, ALU.subtract).then_inc(xq_ready, 1)

        def dve_inner(dve, t, r):
            for c in range(4):
                n = t * 4 + c
                dve.wait_ge(sq_ready, n + 1)
                dve.wait_ge(u_psum, n + 1)
                if c == 0 and not first(t, 2):
                    dve.wait_ge(qi_ready, t - 1)
                nc.vector.tensor_tensor(hin[:, r % 2, c * CH:(c + 1) * CH], ps[:, 4 + c % 2, 0:CH], rel[:, c % 2, :],
                                        ALU.mult).then_inc(h_ready, 1)

        def dve_inner_scale(dve, t, r):
            s, n = r % 2, 6 * t
            h = hm[:, s, :]
            dve.wait_ge(h_ready, t * 4 + 4)
            if not first(t, 2):
                dve.wait_ge(o_ready, t - 1)
                dve.wait_ge(y_ready, t - 1)
            nc.vector.tensor_reduce(h[:, 0:1], hin[:, s, :], AX.X, ALU.max, apply_absolute_value=True)\
                .then_inc(hm_step, 1)
            nc.vector.tensor_scalar(h[:, 1:2], agu[:, s, 1:2], -1.0, None, ALU.mult).then_inc(hm_step, 1)
            dve.wait_ge(hm_step, n + 2)
            nc.vector.tensor_tensor(h[:, 2:3], h[:, 1:2], agu[:, s, 1:2], ALU.max).then_inc(hm_step, 1)
            dve.wait_ge(hm_step, n + 3)
            nc.vector.tensor_scalar(h[:, 3:4], h[:, 0:1], h[:, 2:3], Q_EPS, ALU.mult, ALU.add).then_inc(hm_step, 1)
            nc.vector.tensor_scalar(h[:, 6:7], h[:, 0:1], h[:, 2:3], wfd[:, 0:1], ALU.mult, ALU.mult).then_inc(hm_step, 1)
            dve.wait_ge(hm_step, n + 5)
            nc.vector.reciprocal(h[:, 4:5], h[:, 3:4]).then_inc(hm_step, 1)
            dve.wait_ge(hm_step, n + 6)
            nc.vector.tensor_scalar(h[:, 5:6], h[:, 4:5], agu[:, s, 1:2], 127.0, ALU.mult, ALU.mult).then_inc(hs_ready, 1)

        def dve_inner_quant(dve, t, r):
            dve.wait_ge(y_ready, t + 1)
            if not first(t, 2):
                dve.wait_ge(qt_psum, (t - 1) * 2)
            nc.vector.tensor_scalar(qi[:, r % 2, :], hin[:, r % 2, :], MAGIC, 127.0, ALU.subtract, ALU.min)\
                .then_inc(qi_ready, 1)

        def dve_out(dve, t, r):
            dve.wait_ge(d_psum, t + 1)
            if not first(t, 1):
                dve.wait_ge(out_done[(r - 1) % 4], xr_count(t - 1, (r - 1) % 4))
            nc.vector.scalar_tensor_tensor(out=outt[:, r % 2, :], in0=ps[:, 7, :], scalar=hm[:, r % 2, 6:7],
                                           in1=xr[:, r, :], op0=ALU.mult, op1=ALU.add).then_inc(o_ready, 1)

        def xr_count(t, r):
            return (t - r) * 4 + 16

        @block.vector
        def _(dve):
            dve.wait_ge(consts, 8)
            for j in range(2):
                dve_tiles(dve, j)
            dve.wait_ge(s_psum3, 1)
            nc.vector.tensor_copy(scal[:], ps[:, 7, 32:35]).then_inc(scal_ok, 1)
            dve.wait_ge(scal_ok, 1)
            for w in range(2):
                dve_total(dve, w)
                dve_factor(dve, w)
            for n, w in enumerate((1, 0)):
                for q in range(4):
                    dve_ternary(dve, w, q, 4 * n + q)
            with dve.Fori(2, 4) as j:
                dve_tiles(dve, j)
            for k in range(4 * AHEAD):
                dve_max(dve, 0, k // 32, k % 32)
                if k == 39:
                    dve_rows(dve, 0, 0)
            with dve.Fori(0, SUPERS - 1) as i:
                dve_superunit(dve, i, False)
            dve_superunit(dve, SUPERS - 1, True)
            dve_reciprocal(dve, 0)
            for q in range(4):
                dve_ternary(dve, 2, q, 8 + q)
            nc.vector.tensor_scalar(wfd[:], wfac[:, 2:3], 1.0 / 127.0, None, ALU.mult).then_inc(scal_ok, 1)
            dve.wait_ge(scal_ok, 2)
            dve_reciprocal(dve, 1)
            dve.wait_ge(w_tern, 12)

            def one(tile):
                stage(tile, 1, lambda t, r: dve_x2(dve, t, r))
                stage(tile, 0, lambda t, r: dve_inner(dve, t, r))
                stage(tile, 1, lambda t, r: dve_xh(dve, t, r))
                stage(tile, 0, lambda t, r: dve_inner_scale(dve, t, r))
                stage(tile, 1, lambda t, r: dve_quant(dve, t, r))
                stage(tile, 0, lambda t, r: dve_inner_quant(dve, t, r))
                stage(tile, -1, lambda t, r: dve_out(dve, t, r))
            positions(None, dve, one)

        def cast(out_, in_):
            return nc.gpsimd.tensor_scalar(out_, in_, 1.0, 0.0, ALU.mult, ALU.add)

        def pool_split_job(pool, sup, job):
            n, s = sup * 4 + job, job % 2
            own_wait(pool, job_copy, n + 1)
            if not first(n, 2):
                own_wait(pool, parts_out[s], sup * 96 + 48 * (job // 2))
            cast(spl[:, s, 0, :], qk32[:, s, :]).then_inc(spl_step, 1)
            own_wait(pool, spl_step, n * 4 + 1)
            nc.gpsimd.tensor_tensor(qk32[:, s, :], qk32[:, s, :], spl[:, s, 0, :], ALU.subtract).then_inc(spl_step, 1)
            own_wait(pool, spl_step, n * 4 + 2)
            cast(spl[:, s, 1, :], qk32[:, s, :]).then_inc(spl_step, 1)
            own_wait(pool, spl_step, n * 4 + 3)
            nc.gpsimd.tensor_tensor(qk32[:, s, :], qk32[:, s, :], spl[:, s, 1, :], ALU.subtract).then_inc(spl_step, 1)
            own_wait(pool, spl_step, n * 4 + 4)
            cast(spl[:, s, 2, :], qk32[:, s, :]).then_inc(job_split, 1)

        def pool_split_max(pool, sup, unit):
            s = unit % 2
            n = sup * 16 + unit * 4
            own_wait(pool, nm_ready, sup * 4 + (unit + 1))
            if not (isinstance(sup, int) and sup * 4 + unit < 1):
                own_wait(pool, s_psum, sup * 132 + (rows_at(sup, unit - 1) + 1))
            v = nm[:, s, :].rearrange("p (q h) -> p q h", q=4)
            w = nmr[:, s, :].rearrange("p (q h) -> p q h", q=4)
            cast(nmb[:, :, 0, :], v).then_inc(nm_step, 1)
            own_wait(pool, nm_step, n + 1)
            nc.gpsimd.tensor_tensor(w, v, nmb[:, :, 0, :], ALU.subtract).then_inc(nm_step, 1)
            own_wait(pool, nm_step, n + 2)
            cast(nmb[:, :, 1, :], w).then_inc(nm_step, 1)
            own_wait(pool, nm_step, n + 3)
            nc.gpsimd.tensor_tensor(w, w, nmb[:, :, 1, :], ALU.subtract).then_inc(nm_step, 1)
            own_wait(pool, nm_step, n + 4)
            cast(nmb[:, :, 2, :], w).then_inc(nm_parts, 1)

        def pool_values(pool, sup, set_, batch, group):
            if isinstance(batch, int):
                src = XV[:, 3 - batch, :].rearrange("p (k n) -> p k n", k=KEYT)
            else:
                flat = XV[:, 2:4, :].rearrange("p a n -> p (a n)")
                src = flat[:, bass.ds((1 - batch) * 4096, 4096)].rearrange("p (k n) -> p k n", k=KEYT)
            src = src[:, :, bass.ds(group * P + set_ * 64, 64)].rearrange("p k (h d) -> p k h d", h=GH)
            nc.gpsimd.tensor_copy(Vg[:, set_, :, :, 0:DK], src).then_inc(vg_ready, 1)

        def pool_superunit(pool, sup, batch, group, nbatch, ngroup, last):
            pool_values(pool, sup, 1, batch, group)
            if last:
                own_wait(pool, vg_ready, 2 * SUPERS)
                nc.gpsimd.memset(XV[ILAST:P, 3, 2 * DQ - HID:2 * DQ], 0.0).then_inc(down_zero, 1)
                pool.wait_ge(down_zero, 1)
            for step in range(STEPS):
                if not last and step < 16 and step % 4 == 3:
                    pool_split_job(pool, sup + 1, step // 4)
                if step % KEYT == 4:
                    u = step // KEYT + 1
                    if u < 4:
                        pool_split_max(pool, sup, u)
                    elif not last:
                        pool_split_max(pool, sup + 1, 0)
                if step == 17 and not last:
                    own_wait(pool, av_done, sup * STEPS + 16)
                    pool_values(pool, sup + 1, 0, nbatch, ngroup)
            if not last:
                own_wait(pool, av_done, (sup + 1) * STEPS)

        def pool_att(pool, t, r):
            if isinstance(t, int):
                b, at = t // 8, t % 8 * P
                a, d = num[b][:, :, at:at + P], rdn[:, b, :, at:at + P]
            else:
                b, at = t // 8, (t % 8) * P
                flat = XV[:, 1:3, :].rearrange("p a n -> p (a n)")
                a = flat[:, bass.ds(b * 4096, 4096)].rearrange("p (g t) -> p g t", g=SPB)[:, :, bass.ds(at, P)]
                flat = rdn.rearrange("p b g t -> p (b g t)")
                d = flat[:, bass.ds(b * 4096, 4096)].rearrange("p (g t) -> p g t", g=SPB)[:, :, bass.ds(at, P)]
            if first(t, 1):
                pool.wait_ge(num_in[0], 16)
                pool.wait_ge(rdn_in[0], 64)
                pool.wait_ge(w_tern, 12)
            if first(t, 3) and t == 2:
                pool.wait_ge(num_in[1], 16)
                pool.wait_ge(rdn_in[1], 64)
            if not first(t, 2):
                own_wait(pool, o_psum, t - 1)
            nc.gpsimd.tensor_tensor(att[:, r % 2, :, :], a, d, ALU.mult).then_inc(att_ready, 1)

        def pool_rstd(pool, t, r):
            own_wait(pool, f_stats, t + 1)
            nc.gpsimd.tensor_scalar(vpe[:, r:r + 1], bag[:, r, 1:2], LN_EPS, 1.0, ALU.add, ALU.mult).then_inc(f_var, 1)
            own_wait(pool, f_var, t + 1)
            nc.gpsimd.tensor_tensor(rstd[:, r:r + 1], vpe[:, r:r + 1], expo[:, r:r + 1], ALU.pow).then_inc(f_rs, 1)

        @block.gpsimd
        def _(pool):
            g = nc.gpsimd
            g.memset(ones[:], 1.0).then_inc(consts, 1)
            g.memset(expo[:], -0.5).then_inc(consts, 1)
            g.memset(magic[:], MAGIC).then_inc(consts, 1)
            g.memset(ident[:], 0.0).then_inc(consts, 1)
            g.memset(identb[:], 0.0).then_inc(consts, 1)
            g.memset(Vg[:, :, :, :, :], 1.0).then_inc(consts, 3)
            pool.wait_ge(consts, 8)
            for m in (ident, identb):
                g.affine_select(out=m[:], in_=m[:], compare_op=ALU.not_equal, fill=1.0, base=0,
                                pattern=[[-1, P]], channel_multiplier=1).then_inc(ident_ok, 1)

            def rstds(j):
                own_wait(pool, stats, j + 1)
                if not first(j, 1):
                    own_wait(pool, xn_ready, j * 4)
                g.tensor_scalar(vpe[:], bag[:, :, 1], LN_EPS, 1.0, ALU.add, ALU.mult).then_inc(var_ok, 1)
                own_wait(pool, var_ok, j + 1)
                g.tensor_tensor(rstd[:], vpe[:], expo[:], ALU.pow).then_inc(rs_ready, 1)
            rstds(0)
            rstds(1)
            for job in range(4):
                pool_split_job(pool, 0, job)
            pool.wait_ge(v_copy, 8)
            pool_values(pool, 0, 0, 0, 0)
            pool.wait_ge(w_min, 8)
            pool.wait_ge(vg_ready, 1)
            g.memset(QK[ROWS:AUG, 0, 1, :, :], 1.0).then_inc(ones_set, 1)
            pool.wait_ge(ones_set, 1)
            g.memset(QK[ROWS:AUG, 1, 1, :, :], 1.0).then_inc(ones_set, 1)
            pool.wait_ge(ones_set, 2)
            with pool.Fori(2, 4) as j:
                rstds(j)
            pool_split_max(pool, 0, 0)
            pool.wait_ge(v_copy, TILES)
            with pool.Fori(0, SUPERS - 1) as i:
                pool_superunit(pool, i, i // SPB, i % SPB, (i + 1) // SPB, (i + 1) % SPB, False)
            pool_superunit(pool, SUPERS - 1, 1, SPB - 1, 1, 0, True)

            def one(tile):
                stage(tile, 1, lambda t, r: pool_rstd(pool, t, r))
                stage(tile, 2, lambda t, r: pool_att(pool, t, r))
            positions(None, pool, one)

        def sp_parts_out(sp, sup, job):
            qk, half = job // 2, job % 2
            sp.wait_ge(job_split, sup * 4 + (job + 1))
            for part in range(3):
                dst = parts_d[sup, qk, part * DK:(part + 1) * DK, :, half * HALF:(half + 1) * HALF] if isinstance(sup, int) \
                    else parts_d[bass.ds(sup, 1), qk, part * DK:(part + 1) * DK, :, half * HALF:(half + 1) * HALF].rearrange("a d h t -> (a d) h t")
                sp.dma_start(dst.rearrange("d h t -> h d t"), spl[:, job % 2, part, :]).then_inc(parts_out[job % 2], 16)

        def sp_stack(sp, sup, set_):
            for r in range(2):
                sp.wait_ge(parts_out[r], sup * 96 + 96)
            def part(qk, lo, n):
                if isinstance(sup, int):
                    v = parts_d[sup, qk, lo * DK:(lo + n) * DK, set_ * GH:(set_ + 1) * GH, :]
                else:
                    v = parts_d[bass.ds(sup, 1), qk, lo * DK:(lo + n) * DK, set_ * GH:(set_ + 1) * GH, :].rearrange("a d h t -> (a d) h t")
                return v.rearrange("x h t -> x (h t)")
            def rows(qk, a, n):
                return QK[a * DK:(a + n) * DK, set_, qk, :, :].rearrange("x h t -> x (h t)")
            def load(dst, src):
                sp.dma_start(dst, src).then_inc(stack_in[set_], 16)
            load(rows(0, 0, 3), part(0, 0, 3))
            load(rows(1, 0, 3), part(1, 0, 1).unsqueeze(0).broadcast_to([3, DK, GH * SEQ]))
            load(rows(0, 3, 2), part(0, 0, 2))
            load(rows(1, 3, 2), part(1, 1, 1).unsqueeze(0).broadcast_to([2, DK, GH * SEQ]))
            load(rows(0, 5, 1), part(0, 0, 1))
            load(rows(1, 5, 1), part(1, 2, 1))

        def sp_max_rows(sp, sup, unit):
            set_, half = unit // 2, unit % 2
            sp.wait_ge(s_used, sup * 132 + (rows_at(sup, unit) + 1))
            sp.dma_start(QK[ROWS:AUG, set_, 0, :, half * HALF:(half + 1) * HALF], nmT[:, unit % 2, :])\
                .then_inc(nm_in[half], 16)

        def sp_weights(sp, qk, group):
            w = (wqT, wkT)[qk].rearrange("(k p) n -> p k n", p=P)
            sp.dma_start(wqk[:, qk, :, :], w[:, :, bass.ds(group * P, P)]).then_inc((wq_in, wk_in)[qk], 16)

        def sp_sums_out(sp, sup, batch, group, unit):
            gl, half = unit // 2, unit % 2
            if isinstance(sup, int):
                dst = att_d[batch, :, gl * GH:(gl + 1) * GH, group, half * HALF:(half + 1) * HALF]
            else:
                dst = att_d.rearrange("b x h g t -> b g x h t")[bass.ds(batch, 1), bass.ds(group, 1)]\
                    .rearrange("b g x h t -> (b g x) h t")[:, gl * GH:(gl + 1) * GH, half * HALF:(half + 1) * HALF]
            sp.wait_ge(os_copy, sup * 4 + (unit + 2))
            sp.dma_start(dst.rearrange("x h t -> h x t"), OS[:, unit % 2, :]).then_inc(os_out[unit % 2], 16)

        def sp_superunit(sp, sup, batch, group, ngroup2, last):
            sp_stack(sp, sup, 1)
            if last:
                sp_tail_loads(sp)
            if not last:
                sp_parts_out(sp, sup + 1, 0)
            sp_max_rows(sp, sup, 1)
            if not last:
                sp_parts_out(sp, sup + 1, 1)
                sp_weights(sp, 0, ngroup2)
            sp_sums_out(sp, sup, batch, group, 0)
            if not last:
                sp_parts_out(sp, sup + 1, 2)
            sp_max_rows(sp, sup, 2)
            if not last:
                sp_parts_out(sp, sup + 1, 3)
                sp_weights(sp, 1, ngroup2)
            sp_sums_out(sp, sup, batch, group, 1)
            if not last:
                sp.wait_ge(st_psum, sup * (2 * STEPS) + STEPS)
                sp_stack(sp, sup + 1, 0)
            sp_max_rows(sp, sup, 3)
            sp_sums_out(sp, sup, batch, group, 2)
            if not last:
                sp_max_rows(sp, sup + 1, 0)
            sp_sums_out(sp, sup, batch, group, 3)

        def sp_den_in(sp, b):
            sp.dma_start(den[:, b, :], att_d[b, DK, :, :, :].rearrange("h g (c t) -> (h g c) t", t=256))\
                .then_inc(den_in[b], 16)

        def sp_num_in(sp, b):
            sp.dma_start(num[b], att_d[b, 0:DK].rearrange("x h g t -> (x h) g t")).then_inc(num_in[b], 16)

        def sp_tail_loads(sp):
            sp.wait_ge(job_split, 4 * SUPERS)
            sp.wait_ge(vg_ready, 2 * SUPERS)
            sp_down_loads(sp)
            for g in range(SPB):
                sp.dma_start(wo[:, g, :], woT[g * P:(g + 1) * P, :].rearrange("(h d) n -> d h n", d=DK)).then_inc(wo_in, 16)
            for r in range(2):
                sp.wait_ge(os_out[r], 32 * SPB + 16)
            sp_den_in(sp, 0)
            sp_num_in(sp, 0)

        def sp_down_loads(sp):
            w = wdT[0:(IT - 1) * P, :].rearrange("(k p) n -> p k n", p=P)
            half = 2 * DQ
            for s, c0 in ((0, 0), (3, half)):
                k0, off = c0 // HID, c0 % HID
                dst, src_k, c = XV[:, s, 0:half], k0, 0
                if off:
                    sp.dma_start(dst[:, 0:HID - off], w[:, k0, off:HID]).then_inc(raw_in[2], 16)
                    c, src_k = HID - off, k0 + 1
                n = min((half - c) // HID, IT - 1 - src_k)
                sp.dma_start(dst[:, c:c + n * HID].rearrange("p (k n) -> p k n", n=HID), w[:, src_k:src_k + n, :])\
                    .then_inc(raw_in[2], 16)
                c, src_k = c + n * HID, src_k + n
                if src_k < IT - 1:
                    sp.dma_start(dst[:, c:half], w[:, src_k, 0:half - c]).then_inc(raw_in[2], 16)
                else:
                    sp.dma_start(dst[0:ILAST, c:half], wdT[(IT - 1) * P:, :]).then_inc(raw_in[2], 16)

        @block.sync
        def _(sp):
            for r in range(2):
                sp.sem_inc(os_out[r], 16)
                sp.sem_inc(nm_in[r], 16)
            sp.sem_inc(os_copy, 1)
            xt = x.rearrange("(t p) n -> p t n", p=P)
            for r in range(4):
                sp.dma_start(xin[:, r, :], xt[:, r, :]).then_inc(x_in[r], 16)
                if r == 0:
                    sp.dma_start(wv[:, :, :], wvT.rearrange("(k p) n -> p k n", p=P)).then_inc(wv_in, 16)

            def tiles(j):
                for r in range(4):
                    sp.wait_ge(xn_ready, j * 4 + (r - 3))
                    src = xt[:, j * 4 + r, :] if isinstance(j, int) else xt[:, bass.ds(j * 4 + r, 1), :]
                    dst = xin[:, r, :] if isinstance(j, int) else xin[:, r:r + 1, :]
                    sp.dma_start(dst, src).then_inc(x_in[r], 16)
            sp_weights(sp, 0, 0)
            sp_weights(sp, 1, 0)
            for n, s in enumerate((s_gate, s_up, s_down)):
                sp.dma_start(srow[0:1, n:n + 1], s.rearrange("(a n) -> a n", a=1)).then_inc(s_in, 16)
            tiles(1)
            for w, (src, dst) in enumerate(((wgT, raw_g), (wuT, raw_u))):
                sp.dma_start(dst.rearrange("p (k n) -> p k n", k=KT), src.rearrange("(k p) n -> p k n", p=P))\
                    .then_inc(raw_in[w], 16)
            for job in range(4):
                sp_parts_out(sp, 0, job)
            sp_weights(sp, 0, 1)
            sp_weights(sp, 1, 1)
            with sp.Fori(2, 4) as j:
                tiles(j)
            sp.wait_ge(w_min, 8)
            sp_stack(sp, 0, 0)
            sp.wait_ge(ones_set, 2)
            sp_max_rows(sp, 0, 0)
            with sp.Fori(0, SUPERS - 1) as i:
                sp_superunit(sp, i, i // SPB, i % SPB, (i + 2) % SPB, False)
            sp_superunit(sp, SUPERS - 1, 1, SPB - 1, 0, True)

            def rden(b):
                sp.wait_ge(den_rec, b + 1)
                sp.dma_start(rden_d[b].rearrange("h g (c t) -> (h g c) t", t=256), den[:, b, :]).then_inc(rden_out, 16)
                sp.wait_ge(rden_out, 16 * b + 16)
                for g in range(SPB):
                    sp.dma_start(rdn[:, b, g, :], rden_d[b, :, g, :].unsqueeze(0).broadcast_to([DK, SH, SEQ]))\
                        .then_inc(rdn_in[b], 16)
            for r in range(2):
                sp.dma_start(xr[:, r, :], xt[:, r, :]).then_inc(xr_in[r], 16)
            rden(0)
            for r in range(2):
                sp.wait_ge(os_out[r], 32 * SUPERS + 16)
            sp_den_in(sp, 1)
            sp_num_in(sp, 1)
            rden(1)
            ot = out.rearrange("(t p) n -> p t n", p=P)

            def one(tile):
                def load(t, r):
                    if first(t, 2):
                        return
                    if not first(t, 4):
                        sp.wait_ge(o_ready, t - 3)
                    if isinstance(t, int):
                        sp.dma_start(xr[:, r, :], xt[:, t, :]).then_inc(xr_in[r], 16)
                    else:
                        sp.dma_start(xr[:, r:r + 1, :], xt[:, bass.ds(t, 1), :]).then_inc(xr_in[r], 16)

                def store(t, r):
                    sp.wait_ge(o_ready, t + 1)
                    if isinstance(t, int):
                        sp.dma_start(ot[:, t, :], outt[:, r % 2, :]).then_inc(out_done[r], 16)
                    else:
                        sp.dma_start(ot[:, bass.ds(t, 1), :], outt[:, r % 2:r % 2 + 1, :]).then_inc(out_done[r], 16)
                stage(tile, 2, load)
                stage(tile, -1, store)
            positions(None, sp, one)
            for r in range(4):
                sp.wait_ge(out_done[r], 4 * TILES)


_WEIGHTS = {"wqT": "L0_attn_w_q", "wkT": "L0_attn_w_k", "wvT": "L0_attn_w_v", "woT": "L0_attn_w_o",
            "wgT": "L0_ffn_w_gate", "wuT": "L0_ffn_w_up", "wdT": "L0_ffn_w_down"}
_SCALES = {"s_gate": "L0_ffn_s_gate", "s_up": "L0_ffn_s_up", "s_down": "L0_ffn_s_down"}


def kernel(**inputs):
    import concourse.bacc as bacc
    from concourse.bass_utils import run_bass_kernel_spmd

    x = np.asarray(inputs["L0_attn_x"])
    arrays = {"x": np.ascontiguousarray(x.reshape(TOK, HID))}
    for name, given in _WEIGHTS.items():
        arrays[name] = np.ascontiguousarray(np.asarray(inputs[given]).T)
    for name, given in _SCALES.items():
        arrays[name] = np.ascontiguousarray(inputs[given])
    nc = bacc.Bacc("TRN2", target_bir_lowering=False, num_devices=1)
    args = {name: nc.dram_tensor(name, a.shape, mybir.dt.from_np(a.dtype), kind="ExternalInput").ap()
            for name, a in arrays.items()}
    out = nc.dram_tensor("out", (TOK, HID), F32, kind="ExternalOutput").ap()
    build(nc, out=out, **args)
    r = run_bass_kernel_spmd(nc, [arrays], core_ids=[0])
    return r.results[0]["out"].reshape(BATCH, SEQ, HID)
```

```python
from contextlib import ExitStack

import numpy as np

import concourse.bass as bass
from concourse import mybir

ALU = mybir.AluOpType
ACT = mybir.ActivationFunctionType
AX = mybir.AxisListType
F32 = mybir.dt.float32
BF16 = mybir.dt.bfloat16

P = 128
BATCH, SEQ, HID = 2, 1024, 512
HEADS, DK = 32, 16
INTER = 1376
LN_EPS = 1e-5
Q_EPS = 1e-5
SQRT7 = float(np.sqrt(7.0))
MAGIC = 12582912.0

TOK = BATCH * SEQ
TILES = TOK // P
BT = SEQ // P
KT = HID // P
SH = P // DK
SUPERS = BATCH * HEADS // SH
SPB = HEADS // SH
GH = 4
HALF = 512
KEYT = SEQ // P
STEPS = 4 * KEYT
EARLY_TRANSPOSES = {8: 8, 10: 12}
RAMP_TILE = 3
AHEAD = 11
ROWS = 6 * DK
AUG = ROWS + 3
IT = (INTER + P - 1) // P
ILAST = INTER - (IT - 1) * P
MEAN_BANK = (6, 6, 7)
CH = INTER // 4
WCOL = KT * INTER
DCOL = IT * HID


def build(nc, x, wqT, wkT, wvT, woT, wgT, wuT, wdT, s_gate, s_up, s_down, out):
    ctx = ExitStack()
    with ctx:
        def sb(name, shape, dt):
            return ctx.enter_context(nc.sbuf_tensor(name, shape, dt))

        def sem(name):
            return ctx.enter_context(nc.semaphore(name))

        parts_d = nc.dram_tensor("parts_d", [SUPERS, 2, 3 * DK, SH, SEQ], BF16, kind="Internal").ap()
        att_d = nc.dram_tensor("att_d", [BATCH, 2 * DK, SH, SPB, SEQ], F32, kind="Internal").ap()
        rden_d = nc.dram_tensor("rden_d", [BATCH, SH, SPB, SEQ], F32, kind="Internal").ap()

        XV = sb("XV", [P, 4, 4096], F32)
        QK = sb("QK", [P, 2, 2, GH, SEQ], BF16)
        PB = sb("PB", [P, 2, GH, HALF], F32)
        spl = sb("spl", [P, 2, 3, HALF], BF16)
        qk32 = sb("qk32", [P, 2, HALF], F32)
        Vg = sb("Vg", [P, 2, KEYT, GH, 32], F32)
        wqk = sb("wqk", [P, 2, KT, P], F32)
        wv = sb("wv", [P, KT, HID], F32)
        wo = sb("wo", [P, KT, HID], F32)
        OS = sb("OS", [P, 2, HALF], F32)
        tg = sb("tg", [P, KT, INTER], BF16)
        tu = sb("tu", [P, KT, INTER], BF16)
        td = sb("td", [P, IT, HID], BF16)
        ident = sb("ident", [P, P], F32)
        identb = sb("identb", [P, P], BF16)
        ones = sb("ones", [P, P], F32)
        expo = sb("expo", [P, 4], F32)
        bst = sb("bst", [P, 4, 6], F32)
        bag = sb("bag", [P, 4, 2], F32)
        vpe = sb("vpe", [P, 4], F32)
        rstd = sb("rstd", [P, 4], F32)
        mx = sb("mx", [P, 2, 16, 2], F32)
        nm = sb("nm", [P, 2, 16], F32)
        nmr = sb("nmr", [P, 2, 16], F32)
        nmb = sb("nmb", [P, 4, 3, GH], BF16)
        nmT = sb("nmT", [3 * GH, 2, HALF], BF16)
        wsum = sb("wsum", [P, 3, 4], F32)
        wtot = sb("wtot", [P, 3], F32)
        wmean = sb("wmean", [P, 3], F32)
        wrec = sb("wrec", [P, 3], F32)
        wfac = sb("wfac", [P, 3], F32)
        srow = sb("srow", [1, 3], F32)

        scal = sb("scal", [P, 3], F32)
        wfd = sb("wfd", [P, 1], F32)
        magic = sb("magic", [P, 1], F32)
        bsum = sb("bsum", [P, 2], F32)
        bq = sb("bq", [P, 2, 3], F32)
        agu = sb("agu", [P, 2, 2], F32)
        hm = sb("hm", [P, 2, 8], F32)

        xin = PB[:, 0]
        xnr = PB[:, 1]
        stg = OS[:, :, :].rearrange("p s (k t) -> p s k t", k=KT)
        raw_g = QK[:, :, :, :, :].rearrange("p s q h t -> p (s q h t)").bitcast(F32)[:, 0:WCOL]
        raw_u = XV[:, 1:3, :].rearrange("p a n -> p (a n)")[:, 0:WCOL]
        tern = [tg[:, :, :].rearrange("p k n -> p (k n)"), tu[:, :, :].rearrange("p k n -> p (k n)"),
                td[:, :, :].rearrange("p k n -> p (k n)")]
        DQ = DCOL // 4

        def raw(w, q):
            if w < 2:
                n = WCOL // 4
                return (raw_g, raw_u)[w][:, q * n:(q + 1) * n]
            return XV[:, (0, 3)[q // 2], (q % 2) * DQ:(q % 2 + 1) * DQ]

        def ternq(w, q):
            n = (WCOL, WCOL, DCOL)[w] // 4
            return tern[w][:, q * n:(q + 1) * n]

        num = [XV[:, 1, :].rearrange("p (g t) -> p g t", g=SPB), XV[:, 2, :].rearrange("p (g t) -> p g t", g=SPB)]
        rdn = QK[:, :, :, :, :].rearrange("p s q h t -> p (s q h t)").bitcast(F32).rearrange(
            "p (b g t) -> p b g t", b=BATCH, g=SPB)
        den = qk32[:, :, 0:256]
        xh = XV[:, 0, 0:1024].rearrange("p (s n) -> p s n", s=2)
        att = XV[:, 0, 1024:2048].rearrange("p (s g t) -> p s g t", s=2, g=SPB)
        junk = XV[:, 0, 2048:2560]
        hin = XV[:, 3, 0:2 * INTER].rearrange("p (s n) -> p s n", s=2)
        rel = XV[:, 3, 2 * INTER:2 * INTER + 2 * CH].rearrange("p (s n) -> p s n", s=2)
        xr = PB[:, 0]
        outt = PB[:, 1, 0:2]
        vgb = Vg[:, :, :, :, :].rearrange("p s k h d -> p (s k h d)").bitcast(BF16)
        xq = vgb[:, 0:1024].rearrange("p (s n) -> p s n", s=2)
        xqT = vgb[:, 1024:2048].rearrange("p (s k t) -> p s k t", s=2, k=KT)
        qi = spl[:, :, :, :].rearrange("p s a n -> p (s a n)")[:, 0:2 * INTER].rearrange("p (s n) -> p s n", s=2)
        qiT = wv[:, :, :].rearrange("p k n -> p (k n)").bitcast(BF16)[:, 0:2 * IT * P].rearrange(
            "p (s k t) -> p s k t", s=2, k=IT)

        def xT(region, kt, start, n):
            if isinstance(region, int):
                return XV[:, region, kt * SEQ + start:kt * SEQ + start + n]
            return XV[:, 0:2, :].rearrange("p r n -> p (r n)")[:, bass.ds(region * 4096 + (kt * SEQ + start), n)]

        ps = ctx.enter_context(nc.psum_tensor("ps", [P, 8, 512], F32))

        x_in = [sem(f"x_in{r}") for r in range(4)]
        s_in, wv_in, wo_in, wq_in, wk_in = sem("s_in"), sem("wv_in"), sem("wo_in"), sem("wq_in"), sem("wk_in")
        raw_in = [sem(f"raw_in{w}") for w in range(3)]
        consts, ident_ok = sem("consts"), sem("ident_ok")
        bn_step, stats, var_ok, rs_ready = sem("bn_step"), sem("stats"), sem("var_ok"), sem("rs_ready")
        xn_ready, xt_psum, xt_stg, xt_copy = sem("xn_ready"), sem("xt_psum"), sem("xt_stg"), sem("xt_copy")
        v_psum, v_copy = sem("v_psum"), sem("v_copy")
        w_abs, w_tot, w_psum, w_fac, w_step = sem("w_abs"), sem("w_tot"), sem("w_psum"), sem("w_fac"), sem("w_step")
        w_round, w_min, w_tern, s_psum3 = sem("w_round"), sem("w_min"), sem("w_tern"), sem("s_psum3")
        job_psum, job_copy, job_split, spl_step = sem("job_psum"), sem("job_copy"), sem("job_split"), sem("spl_step")
        parts_out = [sem(f"parts_out{r}") for r in range(2)]
        stack_in = [sem(f"stack_in{s}") for s in range(2)]
        ones_set, vg_ready = sem("ones_set"), sem("vg_ready")
        s_psum, s_used = sem("s_psum"), sem("s_used")
        nm_ready, nm_step, nm_parts = sem("nm_ready"), sem("nm_step"), sem("nm_parts")
        nm_in = [sem(f"nm_in{r}") for r in range(2)]
        st_psum, probs, av_done = sem("st_psum"), sem("probs"), sem("av_done")
        os_copy, os_out = sem("os_copy"), [sem(f"os_out{r}") for r in range(2)]
        den_in = [sem(f"den_in{b}") for b in range(2)]
        num_in = [sem(f"num_in{b}") for b in range(2)]
        rdn_in = [sem(f"rdn_in{b}") for b in range(2)]
        den_rec, rden_out = sem("den_rec"), sem("rden_out")
        xr_in = [sem(f"xr_in{r}") for r in range(4)]
        att_ready, o_psum, x2_ready, f_stats = sem("att_ready"), sem("o_psum"), sem("x2_ready"), sem("f_stats")
        f_bn, f_var, f_rs, xh_ready, x_abs = sem("f_bn"), sem("f_var"), sem("f_rs"), sem("xh_ready"), sem("x_abs")
        q_step, xq_ready, xq_psum, xq_copy = sem("q_step"), sem("xq_ready"), sem("xq_psum"), sem("xq_copy")
        g_psum, u_psum, rel_ready, sq_ready = sem("g_psum"), sem("u_psum"), sem("rel_ready"), sem("sq_ready")
        h_ready, hm_step, hs_ready, y_ready, qi_ready = (sem("h_ready"), sem("hm_step"), sem("hs_ready"),
                                                         sem("y_ready"), sem("qi_ready"))
        qt_psum, qt_copy, d_psum, o_ready = sem("qt_psum"), sem("qt_copy"), sem("d_psum"), sem("o_ready")
        out_done = [sem(f"out_done{r}") for r in range(4)]
        scal_ok, down_zero, waits_carried = sem("scal_ok"), sem("down_zero"), sem("waits_carried")
        block = ctx.enter_context(nc.Block())

        def own_wait(eng, semaphore, value):
            eng.wait_ge(semaphore, value)
            eng.sem_inc(waits_carried, 1)

        def first(n, limit):
            return isinstance(n, int) and n < limit

        def item_at(sup, unit, k):
            rest = 33 * unit + k - (1 if k < 8 and not (first(sup, 1) and unit == 0) else 0)
            return rest

        def rows_at(sup, unit):
            return 33 * unit + (40 if not (isinstance(sup, int) and sup == SUPERS - 1 and unit == 3) else 32)

        def step_items(step):
            found = []
            for j in range(4):
                n = (step + AHEAD) * 4 + j
                found.append((n // 128, n % 128 // 32, n % 32))
            return found

        def rows_unit(step):
            if step % KEYT != 6:
                return None
            u = step // KEYT + 1
            return (u // 4, u % 4)

        def pe_tile_transpose(pe, t):
            pe.wait_ge(xn_ready, t + 1)
            if t >= 2:
                pe.wait_ge(xt_copy, t - 1)
            for k in range(KT):
                last = nc.tensor.transpose(ps[:, t % 2, k * P:(k + 1) * P], xnr[:, t % 4, k * P:(k + 1) * P], ident[:])
            last.then_inc(xt_psum, 1)

        def pe_tile_values(pe, t, k):
            if k == 0:
                if t == 0:
                    pe.wait_ge(wv_in, 16)
                if t in EARLY_TRANSPOSES or t == 0:
                    pe.wait_ge(xt_copy, (BT if t == 0 else EARLY_TRANSPOSES[t] + 4))
                if t >= 2:
                    pe.wait_ge(v_copy, t - 1)
            last = nc.tensor.matmul(ps[:, 2 + t % 2, :], xT(t // BT, k, t % BT * P, P), wv[:, k, :],
                                    start=(k == 0), stop=(k == KT - 1))
            if k == KT - 1:
                last.then_inc(v_psum, 1)

        def pe_mean(pe, w):
            pe.wait_ge(w_tot, w + 1)
            nc.tensor.matmul(ps[:, MEAN_BANK[w], 8 * w:8 * w + 1], ones[:], wtot[:, w:w + 1], start=True, stop=True)\
                .then_inc(w_psum, 1)

        def pe_job(pe, sup, region, job, k):
            qk, half = job // 2, job % 2
            n = sup * 4 + job
            if k == 0:
                if half == 0:
                    pe.wait_ge((wq_in, wk_in)[qk], sup * 16 + 16)
                if not first(n, 1):
                    pe.wait_ge(job_copy, n)
            last = nc.tensor.matmul(ps[:, 7, :], wqk[:, qk, k, :], xT(region, k, half * HALF, HALF),
                                    start=(k == 0), stop=(k == KT - 1))
            if k == KT - 1:
                last.then_inc(job_psum, 1)

        def pe_scores(pe, sup, unit, k):
            slot, j = k // 4, k % 4
            qt, head, kh = slot // 2, (slot % 2) * 2 + j // 2, j % 2
            set_, half = unit // 2, unit % 2
            at = item_at(sup, unit, k)
            if k == 0 and half == 0:
                pe.wait_ge(stack_in[set_], sup * 96 + 96)
            if not (isinstance(sup, int) and sup * 132 + at < 2):
                pe.wait_ge(s_used, sup * 132 + (at - 1))
            nc.tensor.matmul(ps[:, 4 + at % 2, :],
                             QK[0:ROWS, set_, 0, head, half * HALF + qt * P:half * HALF + (qt + 1) * P],
                             QK[0:ROWS, set_, 1, head, kh * HALF:(kh + 1) * HALF],
                             start=True, stop=True).then_inc(s_psum, 1)

        def pe_max_rows(pe, sup, unit):
            at = rows_at(sup, unit)
            pe.wait_ge(nm_parts, sup * 4 + (unit + 1))
            pe.wait_ge(s_used, sup * 132 + (at - 1))
            dst = ps[0:3 * GH, 4 + at % 2, :].bitcast(BF16)
            for qt in range(4):
                last = nc.tensor.transpose(dst[:, qt * P:(qt + 1) * P],
                                           nmb[:, qt, :, :].rearrange("p a h -> p (a h)"), identb[:])
            last.then_inc(s_psum, 1)

        def pe_scoresT(pe, sup, step, pair):
            unit, kt = step // KEYT, step % KEYT
            set_, half = unit // 2, unit % 2
            if kt == 0 and pair == 0:
                pe.wait_ge(nm_in[half], sup * 32 + 16 * (set_ + 2))
            if step > 0:
                pe.wait_ge(probs, sup * (2 * STEPS) + (2 * step + pair - 1))
            for h2 in range(2):
                head = pair * 2 + h2
                last = nc.tensor.matmul(ps[:, 2 * pair + h2, :], QK[0:AUG, set_, 1, head, kt * P:(kt + 1) * P],
                                        QK[0:AUG, set_, 0, head, half * HALF:(half + 1) * HALF],
                                        start=True, stop=True)
            last.then_inc(st_psum, 1)

        def pe_av(pe, sup, step, part):
            unit, kt = step // KEYT, step % KEYT
            set_ = unit // 2
            if part == 0:
                pe.wait_ge(probs, sup * (2 * STEPS) + (2 * step + 2))
            if kt == 0 and part == 0:
                if unit % 2 == 0:
                    pe.wait_ge(vg_ready, sup * 2 + (set_ + 1))
                pe.wait_ge(os_copy, sup * 4 + (unit + 1))
            for h in range(GH):
                last = nc.tensor.matmul(ps[32 * h:32 * h + 32, 6, part * 256:part * 256 + 256], Vg[:, set_, kt, h, :],
                                        PB[:, step % 2, h, part * 256:part * 256 + 256],
                                        start=(kt == 0 and part == 0), stop=(kt == KEYT - 1 and part == 1))
            if part == 1:
                last.then_inc(av_done, 1)

        def pe_superunit(pe, sup, region, last):
            for step in range(STEPS):
                items = [(lambda a=a, u=u, k=k: pe_scores(pe, sup + a, u, k)) if not (last and a) else (lambda: None)
                         for a, u, k in step_items(step)]
                items[0]()
                pe_scoresT(pe, sup, step, 0)
                items[1]()
                pe_scoresT(pe, sup, step, 1)
                items[2]()
                if step > 0:
                    pe_av(pe, sup, step - 1, 0)
                items[3]()
                if step > 0:
                    pe_av(pe, sup, step - 1, 1)
                if not last and step < 16:
                    pe_job(pe, sup + 1, region, step // 4, step % 4)
                rows = rows_unit(step)
                if rows and not (last and rows[0]):
                    pe_max_rows(pe, sup + rows[0], rows[1])
                if last and step == 20:
                    pe_mean(pe, 2)
            pe_av(pe, sup, STEPS - 1, 0)
            pe_av(pe, sup, STEPS - 1, 1)

        def pe_attention_out(pe, t, r):
            pe.wait_ge(att_ready, t + 1)
            if not first(t, 1):
                pe.wait_ge(x2_ready, t)
            for g in range(SPB):
                last = nc.tensor.matmul(ps[:, 0, :], att[:, r % 2, g, :], wo[:, g, :],
                                        start=(g == 0), stop=(g == SPB - 1))
            last.then_inc(o_psum, 1)

        def pe_xq_transpose(pe, t, r):
            pe.wait_ge(xq_ready, t + 1)
            if not first(t, 2):
                pe.wait_ge(qt_copy, (t - 1) * 2)
            dst = ps[:, 1, :].bitcast(BF16)
            for k in range(KT):
                last = nc.tensor.transpose(dst[:, k * P:(k + 1) * P], xq[:, r % 2, k * P:(k + 1) * P], identb[:])
            last.then_inc(xq_psum, 1)

        def pe_gate_up(pe, t, r):
            pe.wait_ge(xq_copy, t + 1)
            for c in range(4):
                n = t * 4 + c
                for w, bank, ready, used in ((tg, 2, g_psum, rel_ready), (tu, 4, u_psum, h_ready)):
                    if not first(n, 2):
                        pe.wait_ge(used, n - 1)
                    for k in range(KT):
                        last = nc.tensor.matmul(ps[:, bank + c % 2, 0:CH], xqT[:, r % 2, k, :],
                                                w[:, k, c * CH:(c + 1) * CH], start=(k == 0), stop=(k == KT - 1))
                    last.then_inc(ready, 1)

        def pe_inner_transpose(pe, t, r):
            pe.wait_ge(qi_ready, t + 1)
            if not first(t, 1):
                pe.wait_ge(qt_copy, t * 2)
            for k in range(IT):
                n = P if k < IT - 1 else ILAST
                dst = ps[:, 6, :].bitcast(BF16)[0:n, k * P:(k + 1) * P] if k < 8 else \
                    ps[:, 1, :].bitcast(BF16)[0:n, (k - 4) * P:(k - 3) * P]
                last = nc.tensor.transpose(dst, qi[:, r % 2, k * P:k * P + n], identb[:])
                if k in (7, IT - 1):
                    last.then_inc(qt_psum, 1)

        def pe_down(pe, t, r):
            pe.wait_ge(qt_copy, t * 2 + 2)
            if not first(t, 1):
                pe.wait_ge(o_ready, t)
            for k in range(IT):
                n = P if k < IT - 1 else ILAST
                last = nc.tensor.matmul(ps[:, 7, :], qiT[0:n, r % 2, k, :], td[0:n, k, :],
                                        start=(k == 0), stop=(k == IT - 1))
            last.then_inc(d_psum, 1)

        def positions(run, eng, one):
            def at(p, r):
                def tile(delta):
                    t = p + delta
                    return (t, (r + delta) % 4) if not isinstance(t, int) or 0 <= t < TILES else None
                one(tile)
            for p in (-2, -1, 0, 1):
                at(p, p % 4)
            with eng.Fori(0, 3) as m:
                for r in range(4):
                    at(m * 4 + (2 + r), (2 + r) % 4)
            for p in (14, 15, 16):
                at(p, p % 4)

        def stage(tile, delta, do, *more):
            found = tile(delta)
            if found:
                do(*found)

        @block.tensor
        def _(pe):
            pe.wait_ge(consts, 8)
            pe.wait_ge(ident_ok, 2)
            for t in range(BT):
                pe_tile_transpose(pe, t)
            pe.wait_ge(s_in, 48)
            nc.tensor.matmul(ps[:, 6, 32:35], ones[0:1, :], srow[:], start=True, stop=True).then_inc(s_psum3, 1)
            pe_mean(pe, 0)
            pe.wait_ge(xt_copy, BT)
            for job in range(4):
                for k in range(KT):
                    pe_job(pe, 0, 0, job, k)
            item = 0
            for t in range(TILES):
                if t in EARLY_TRANSPOSES:
                    for n in range(4):
                        pe_tile_transpose(pe, EARLY_TRANSPOSES[t] + n)
                for k in range(KT):
                    pe_tile_values(pe, t, k)
                    if t >= RAMP_TILE and item < 4 * AHEAD:
                        pe_scores(pe, 0, item // 32, item % 32)
                        item += 1
                        if item == 40:
                            pe_max_rows(pe, 0, 0)
                if t == 1:
                    pe_mean(pe, 1)
            pe.wait_ge(w_fac, 2)
            pe.wait_ge(v_copy, TILES)
            with pe.Fori(0, SUPERS - 1) as i:
                pe_superunit(pe, i, (i + 1) // SPB, False)
            pe_superunit(pe, SUPERS - 1, 1, True)
            pe.wait_ge(os_copy, 4 * SUPERS + 1)
            pe.wait_ge(s_used, 132 * SUPERS)
            pe.wait_ge(wo_in, 64)
            pe.wait_ge(w_tern, 12)
            pe.wait_ge(w_fac, 3)

            def one(tile):
                stage(tile, 0, lambda t, r: pe_gate_up(pe, t, r))
                stage(tile, -1, lambda t, r: pe_inner_transpose(pe, t, r))
                stage(tile, 2, lambda t, r: pe_attention_out(pe, t, r))
                stage(tile, -1, lambda t, r: pe_down(pe, t, r))
                stage(tile, 1, lambda t, r: pe_xq_transpose(pe, t, r))
            positions(None, pe, one)

        def act_tile_copy(act, t):
            b = t // BT
            if t == BT:
                act.wait_ge(w_min, 8)
            act.wait_ge(xt_psum, t + 1)
            dst = XV[:, b, :].rearrange("p (k t) -> p k t", k=KT)[:, :, t % BT * P:(t % BT + 1) * P]
            nc.scalar.activation(dst, ps[:, t % 2, :].rearrange("p (k t) -> p k t", k=KT), ACT.Copy).then_inc(xt_copy, 1)

        def act_value_copy(act, t):
            act.wait_ge(v_psum, t + 1)
            nc.scalar.activation(XV[:, 3 - t // BT, t % BT * HID:(t % BT + 1) * HID], ps[:, 2 + t % 2, :], ACT.Copy)\
                .then_inc(v_copy, 1)

        def act_job(act, sup, job):
            n = sup * 4 + job
            act.wait_ge(job_psum, n + 1)
            if not first(n, 2):
                act.wait_ge(job_split, n - 1)
            nc.scalar.activation(qk32[:, job % 2, :], ps[:, 7, :], ACT.Copy).then_inc(job_copy, 1)

        def act_abs(act, w, q):
            if q == 0:
                act.wait_ge(raw_in[w], 16 * (1, 1, 5)[w])
                if w == 2:
                    act.wait_ge(down_zero, 1)
            nc.scalar.activation(ternq(w, q), raw(w, q), ACT.Abs, accum_out=wsum[:, w, q:q + 1]).then_inc(w_abs, 1)

        def act_round(act, w, q):
            if q == 0:
                act.wait_ge(w_fac, w + 1)
            act.wait_ge(w_abs, 4 * w + q + 1)
            nc.scalar.activation(raw(w, q), raw(w, q), ACT.Identity, bias=magic[:], scale=wrec[:, w:w + 1])\
                .then_inc(w_round, 1)

        def act_exp(act, sup, step, pair):
            n = 2 * step + pair
            act.wait_ge(st_psum, sup * (2 * STEPS) + (n + 1))
            if pair == 0 and step > 1:
                act.wait_ge(av_done, sup * STEPS + (step - 1))
            nc.scalar.activation(PB[:, step % 2, 2 * pair:2 * pair + 2, :], ps[:, 2 * pair:2 * pair + 2, :],
                                 ACT.Exp, scale=1.0 / float(np.sqrt(DK))).then_inc(probs, 1)

        def act_sums(act, sup, unit):
            act.wait_ge(av_done, sup * STEPS + KEYT * (unit + 1))
            act.wait_ge(os_out[unit % 2], sup * 32 + 16 * (unit // 2 + 1))
            nc.scalar.activation(OS[:, unit % 2, :], ps[:, 6, :], ACT.Copy).then_inc(os_copy, 1)

        def act_superunit(act, sup, last):
            for step in range(STEPS):
                act_exp(act, sup, step, 0)
                act_exp(act, sup, step, 1)
                if step % KEYT == 0 and step > 0:
                    act_sums(act, sup, step // KEYT - 1)
                if not last and step < 16 and step % 4 == 3:
                    act_job(act, sup + 1, step // 4)
                if last and step in (12, 14, 16, 18):
                    act_abs(act, 2, (step - 12) // 2)
                if last and step in (23, 25, 27, 29):
                    act_round(act, 2, (step - 23) // 2)
            act_sums(act, sup, 3)

        def act_abs_x(act, t, r):
            act.wait_ge(xh_ready, t + 1)
            if not first(t, 2):
                act.wait_ge(xq_ready, t - 1)
            if not first(t, 1):
                act.wait_ge(x_abs, t)
            nc.scalar.activation(junk, xh[:, r % 2, :], ACT.Abs, accum_out=bsum[:, r % 2:r % 2 + 1]).then_inc(x_abs, 1)

        def act_xq_copy(act, t, r):
            act.wait_ge(xq_psum, t + 1)
            if not first(t, 2):
                act.wait_ge(u_psum, (t - 1) * 4)
            nc.scalar.activation(xqT[:, r % 2].rearrange("p k t -> p (k t)"), ps[:, 1, :].bitcast(BF16)[:, 0:HID],
                                 ACT.Copy).then_inc(xq_copy, 1)

        def act_gate(act, t, r):
            for c in range(4):
                n = t * 4 + c
                act.wait_ge(g_psum, n + 1)
                if not first(n, 2):
                    act.wait_ge(h_ready, n - 1)
                nc.scalar.activation(rel[:, c % 2, :], ps[:, 2 + c % 2, 0:CH], ACT.Relu,
                                     scale=agu[:, r % 2, 0:1]).then_inc(rel_ready, 1)
                act.wait_ge(rel_ready, n + 1)
                nc.scalar.activation(rel[:, c % 2, :], rel[:, c % 2, :], ACT.Square).then_inc(sq_ready, 1)

        def act_inner_round(act, t, r):
            act.wait_ge(hs_ready, t + 1)
            nc.scalar.activation(hin[:, r % 2, :], hin[:, r % 2, :], ACT.Identity, bias=magic[:],
                                 scale=hm[:, r % 2, 5:6]).then_inc(y_ready, 1)

        def act_inner_copy(act, t, r):
            act.wait_ge(qt_psum, t * 2 + 1)
            if not first(t, 1):
                act.wait_ge(d_psum, t)
            nc.scalar.activation(qiT[:, r % 2, 0:8, :].rearrange("p k t -> p (k t)"), ps[:, 6, :].bitcast(BF16),
                                 ACT.Copy).then_inc(qt_copy, 1)
            act.wait_ge(qt_psum, t * 2 + 2)
            src = ps[:, 1, :].bitcast(BF16)
            nc.scalar.activation(qiT[:, r % 2, 8:10, :].rearrange("p k t -> p (k t)"), src[:, 4 * P:6 * P], ACT.Copy)
            nc.scalar.activation(qiT[0:ILAST, r % 2, 10, :], src[0:ILAST, 6 * P:7 * P], ACT.Copy).then_inc(qt_copy, 1)

        @block.scalar
        def _(act):
            act.wait_ge(consts, 8)
            for t in range(BT):
                act_tile_copy(act, t)
                if t in (3, 4, 5, 6):
                    act_abs(act, 0, t - 3)
            for job in range(4):
                act_round(act, 0, job)
                act_job(act, 0, job)
                act_abs(act, 1, job)
            for t in range(TILES):
                if t in EARLY_TRANSPOSES:
                    for n in range(4):
                        act_tile_copy(act, EARLY_TRANSPOSES[t] + n)
                act_value_copy(act, t)
                if t in (1, 2):
                    act_round(act, 1, 2 * t - 2)
                    act_round(act, 1, 2 * t - 1)
            with act.Fori(0, SUPERS - 1) as i:
                act_superunit(act, i, False)
            act_superunit(act, SUPERS - 1, True)
            act.wait_ge(w_tern, 12)

            def one(tile):
                stage(tile, 0, lambda t, r: act_gate(act, t, r))
                stage(tile, -1, lambda t, r: act_inner_copy(act, t, r))
                stage(tile, 1, lambda t, r: act_abs_x(act, t, r))
                stage(tile, 0, lambda t, r: act_inner_round(act, t, r))
                stage(tile, 1, lambda t, r: act_xq_copy(act, t, r))
            positions(None, act, one)

        def dve_bn(dve, t):
            dve.wait_ge(x_in[t % 4], t // 4 * 16 + 16)
            if t >= 4:
                dve.wait_ge(stats, t // 4)
            nc.vector.bn_stats(bst[:, t % 4, :], xin[:, t % 4, :]).then_inc(bn_step, 1)

        def dve_stats(dve, j):
            dve.wait_ge(bn_step, j * 4 + 4)
            if j > 0:
                dve.wait_ge(xn_ready, j * 4)
            for r in range(4):
                last = nc.vector.bn_aggr(bag[:, r, :], bst[:, r, :])
            last.then_inc(stats, 1)

        def dve_normalise(dve, t):
            if t % 4 == 0:
                dve.wait_ge(stats, t // 4 + 1)
                dve.wait_ge(rs_ready, t // 4 + 1)
            if t >= 4:
                dve.wait_ge(xt_psum, t - 3)
            nc.vector.tensor_scalar(xnr[:, t % 4, :], xin[:, t % 4, :], bag[:, t % 4, 0:1], rstd[:, t % 4:t % 4 + 1],
                                    ALU.subtract, ALU.mult).then_inc(xn_ready, 1)

        def dve_tiles(dve, j):
            for r in range(4):
                dve_bn(dve, j * 4 + r)
            dve_stats(dve, j)
            for r in range(4):
                dve_normalise(dve, j * 4 + r)

        def dve_total(dve, w):
            dve.wait_ge(w_abs, 4 * w + 4)
            nc.vector.reduce_sum(wtot[:, w:w + 1], wsum[:, w, :], AX.X).then_inc(w_tot, 1)

        def dve_factor(dve, w):
            dve.wait_ge(w_psum, w + 1)
            nc.vector.tensor_scalar(wmean[:, w:w + 1], ps[:, MEAN_BANK[w], 8 * w:8 * w + 1], 1.0 / (INTER * HID), None, ALU.mult)\
                .then_inc(w_step, 1)
            dve.wait_ge(w_step, 3 * w + 1)
            nc.vector.tensor_scalar(wrec[:, w:w + 1], wmean[:, w:w + 1], Q_EPS, None, ALU.add).then_inc(w_step, 1)
            nc.vector.tensor_tensor(wfac[:, w:w + 1], scal[:, w:w + 1], wmean[:, w:w + 1], ALU.mult)\
                .then_inc(w_step, 1)
            dve.wait_ge(w_step, 3 * w + 3)
            nc.vector.reciprocal(wrec[:, w:w + 1], wrec[:, w:w + 1]).then_inc(w_fac, 1)

        def dve_ternary(dve, w, q, order):
            dve.wait_ge(w_round, order + 1)
            nc.vector.tensor_scalar(ternq(w, q), raw(w, q), MAGIC, 1.0, ALU.subtract, ALU.min).then_inc(w_min, 1)
            dve.wait_ge(w_min, order + 1)
            nc.vector.tensor_scalar(ternq(w, q), ternq(w, q), -1.0, None, ALU.max).then_inc(w_tern, 1)

        def dve_max(dve, sup, unit, k):
            slot, j = k // 4, k % 4
            qt, head, kh = slot // 2, (slot % 2) * 2 + j // 2, j % 2
            at = item_at(sup, unit, k)
            dve.wait_ge(s_psum, sup * 132 + (at + 1))
            if k == 0 and not (isinstance(sup, int) and sup * 4 + unit < 2):
                dve.wait_ge(nm_ready, sup * 4 + (unit - 1))
            nc.vector.tensor_reduce(mx[:, unit % 2, qt * 4 + head, kh:kh + 1], ps[:, 4 + at % 2, :], AX.X, ALU.max)\
                .then_inc(s_used, 1)
            if k == 31:
                dve.wait_ge(s_used, sup * 132 + (at + 1))
                if not (isinstance(sup, int) and sup * 4 + unit < 1):
                    dve.wait_ge(nm_parts, sup * 4 + unit)
                nc.vector.tensor_reduce(nm[:, unit % 2, :], mx[:, unit % 2, :, :], AX.X, ALU.max, negate=True)\
                    .then_inc(nm_ready, 1)

        def dve_rows(dve, sup, unit):
            at = rows_at(sup, unit)
            dve.wait_ge(s_psum, sup * 132 + (at + 1))
            dve.wait_ge(nm_in[unit % 2], sup * 32 + 16 * (unit // 2 + 1))
            nc.vector.tensor_copy(nmT[:, unit % 2, :], ps[0:3 * GH, 4 + at % 2, :].bitcast(BF16)[:, 0:HALF])\
                .then_inc(s_used, 1)

        def dve_superunit(dve, sup, last):
            for step in range(STEPS):
                for a, u, k in step_items(step):
                    if not (last and a):
                        dve_max(dve, sup + a, u, k)
                rows = rows_unit(step)
                if rows and not (last and rows[0]):
                    dve_rows(dve, sup + rows[0], rows[1])
                if last and step == 20:
                    dve_total(dve, 2)
                    dve_factor(dve, 2)

        def dve_reciprocal(dve, b):
            dve.wait_ge(den_in[b], 16)
            nc.vector.reciprocal(den[:, b, :], den[:, b, :]).then_inc(den_rec, 1)

        def dve_x2(dve, t, r):
            dve.wait_ge(o_psum, t + 1)
            dve.wait_ge(xr_in[r], xr_count(t, r))
            nc.vector.tensor_tensor(xr[:, r, :], ps[:, 0, :], xr[:, r, :], ALU.add).then_inc(x2_ready, 1)
            dve.wait_ge(x2_ready, t + 1)
            nc.vector.bn_stats(bst[:, r, :], xr[:, r, :]).then_inc(f_bn, 1)
            own_wait(dve, f_bn, t + 1)
            nc.vector.bn_aggr(bag[:, r, :], bst[:, r, :]).then_inc(f_stats, 1)

        def dve_xh(dve, t, r):
            dve.wait_ge(f_rs, t + 1)
            if not first(t, 2):
                dve.wait_ge(xq_ready, t - 1)
            nc.vector.tensor_scalar(xh[:, r % 2, :], xr[:, r, :], bag[:, r, 0:1], rstd[:, r:r + 1],
                                    ALU.subtract, ALU.mult).then_inc(xh_ready, 1)

        def dve_quant(dve, t, r):
            s = r % 2
            n = 5 * t
            dve.wait_ge(x_abs, t + 1)
            nc.vector.tensor_scalar(bq[:, s, 0:1], bsum[:, s:s + 1], 1.0 / HID, Q_EPS, ALU.mult, ALU.add)\
                .then_inc(q_step, 1)
            if not first(t, 2):
                dve.wait_ge(hs_ready, t - 1)
            nc.vector.tensor_scalar(agu[:, s, :], wfac[:, 0:2], bsum[:, s:s + 1], 1.0 / HID, ALU.mult, ALU.mult)
            dve.wait_ge(q_step, n + 1)
            nc.vector.reciprocal(bq[:, s, 1:2], bq[:, s, 0:1]).then_inc(q_step, 1)
            dve.wait_ge(q_step, n + 2)
            nc.vector.tensor_scalar(bq[:, s, 2:3], bq[:, s, 1:2], SQRT7, None, ALU.mult).then_inc(q_step, 1)
            dve.wait_ge(q_step, n + 3)
            nc.vector.tensor_scalar(xh[:, s, :], xh[:, s, :], bq[:, s, 2:3], 7.0, ALU.mult, ALU.min).then_inc(q_step, 1)
            dve.wait_ge(q_step, n + 4)
            nc.vector.tensor_scalar(xh[:, s, :], xh[:, s, :], -8.0, MAGIC, ALU.max, ALU.add).then_inc(q_step, 1)
            dve.wait_ge(q_step, n + 5)
            if not first(t, 2):
                dve.wait_ge(xq_psum, t - 1)
            nc.vector.tensor_scalar(xq[:, s, :], xh[:, s, :], MAGIC, None, ALU.subtract).then_inc(xq_ready, 1)

        def dve_inner(dve, t, r):
            for c in range(4):
                n = t * 4 + c
                dve.wait_ge(sq_ready, n + 1)
                dve.wait_ge(u_psum, n + 1)
                if c == 0 and not first(t, 2):
                    dve.wait_ge(qi_ready, t - 1)
                nc.vector.tensor_tensor(hin[:, r % 2, c * CH:(c + 1) * CH], ps[:, 4 + c % 2, 0:CH], rel[:, c % 2, :],
                                        ALU.mult).then_inc(h_ready, 1)

        def dve_inner_scale(dve, t, r):
            s, n = r % 2, 6 * t
            h = hm[:, s, :]
            dve.wait_ge(h_ready, t * 4 + 4)
            if not first(t, 2):
                dve.wait_ge(o_ready, t - 1)
                dve.wait_ge(y_ready, t - 1)
            nc.vector.tensor_reduce(h[:, 0:1], hin[:, s, :], AX.X, ALU.max, apply_absolute_value=True)\
                .then_inc(hm_step, 1)
            nc.vector.tensor_scalar(h[:, 1:2], agu[:, s, 1:2], -1.0, None, ALU.mult).then_inc(hm_step, 1)
            dve.wait_ge(hm_step, n + 2)
            nc.vector.tensor_tensor(h[:, 2:3], h[:, 1:2], agu[:, s, 1:2], ALU.max).then_inc(hm_step, 1)
            dve.wait_ge(hm_step, n + 3)
            nc.vector.tensor_scalar(h[:, 3:4], h[:, 0:1], h[:, 2:3], Q_EPS, ALU.mult, ALU.add).then_inc(hm_step, 1)
            nc.vector.tensor_scalar(h[:, 6:7], h[:, 0:1], h[:, 2:3], wfd[:, 0:1], ALU.mult, ALU.mult).then_inc(hm_step, 1)
            dve.wait_ge(hm_step, n + 5)
            nc.vector.reciprocal(h[:, 4:5], h[:, 3:4]).then_inc(hm_step, 1)
            dve.wait_ge(hm_step, n + 6)
            nc.vector.tensor_scalar(h[:, 5:6], h[:, 4:5], agu[:, s, 1:2], 127.0, ALU.mult, ALU.mult).then_inc(hs_ready, 1)

        def dve_inner_quant(dve, t, r):
            dve.wait_ge(y_ready, t + 1)
            if not first(t, 2):
                dve.wait_ge(qt_psum, (t - 1) * 2)
            nc.vector.tensor_scalar(qi[:, r % 2, :], hin[:, r % 2, :], MAGIC, 127.0, ALU.subtract, ALU.min)\
                .then_inc(qi_ready, 1)

        def dve_out(dve, t, r):
            dve.wait_ge(d_psum, t + 1)
            if not first(t, 1):
                dve.wait_ge(out_done[(r - 1) % 4], xr_count(t - 1, (r - 1) % 4))
            nc.vector.scalar_tensor_tensor(out=outt[:, r % 2, :], in0=ps[:, 7, :], scalar=hm[:, r % 2, 6:7],
                                           in1=xr[:, r, :], op0=ALU.mult, op1=ALU.add).then_inc(o_ready, 1)

        def xr_count(t, r):
            return (t - r) * 4 + 16

        @block.vector
        def _(dve):
            dve.wait_ge(consts, 8)
            for j in range(2):
                dve_tiles(dve, j)
            dve.wait_ge(s_psum3, 1)
            nc.vector.tensor_copy(scal[:], ps[:, 6, 32:35]).then_inc(scal_ok, 1)
            dve.wait_ge(scal_ok, 1)
            for w in range(2):
                dve_total(dve, w)
                dve_factor(dve, w)
                if w == 1:
                    dve_tiles(dve, 2)
                for q in range(4):
                    dve_ternary(dve, w, q, 4 * w + q)
            for k in range(4 * AHEAD):
                dve_max(dve, 0, k // 32, k % 32)
                if k in (15, 16, 17, 18):
                    dve_bn(dve, k - 3)
                if k == 19:
                    dve_stats(dve, 3)
                if k in (20, 21, 22, 23):
                    dve_normalise(dve, k - 8)
                if k == 39:
                    dve_rows(dve, 0, 0)
            with dve.Fori(0, SUPERS - 1) as i:
                dve_superunit(dve, i, False)
            dve_superunit(dve, SUPERS - 1, True)
            dve_reciprocal(dve, 0)
            for q in range(4):
                dve_ternary(dve, 2, q, 8 + q)
            nc.vector.tensor_scalar(wfd[:], wfac[:, 2:3], 1.0 / 127.0, None, ALU.mult).then_inc(scal_ok, 1)
            dve.wait_ge(scal_ok, 2)
            dve_reciprocal(dve, 1)
            dve.wait_ge(w_tern, 12)

            def one(tile):
                stage(tile, 1, lambda t, r: dve_x2(dve, t, r))
                stage(tile, 0, lambda t, r: dve_inner(dve, t, r))
                stage(tile, 1, lambda t, r: dve_xh(dve, t, r))
                stage(tile, 0, lambda t, r: dve_inner_scale(dve, t, r))
                stage(tile, 1, lambda t, r: dve_quant(dve, t, r))
                stage(tile, 0, lambda t, r: dve_inner_quant(dve, t, r))
                stage(tile, -1, lambda t, r: dve_out(dve, t, r))
            positions(None, dve, one)

        def cast(out_, in_):
            return nc.gpsimd.tensor_scalar(out_, in_, 1.0, 0.0, ALU.mult, ALU.add)

        def pool_split_job(pool, sup, job):
            n, s = sup * 4 + job, job % 2
            own_wait(pool, job_copy, n + 1)
            if not first(n, 2):
                own_wait(pool, parts_out[s], sup * 96 + 48 * (job // 2))
            cast(spl[:, s, 0, :], qk32[:, s, :]).then_inc(spl_step, 1)
            own_wait(pool, spl_step, n * 4 + 1)
            nc.gpsimd.tensor_tensor(qk32[:, s, :], qk32[:, s, :], spl[:, s, 0, :], ALU.subtract).then_inc(spl_step, 1)
            own_wait(pool, spl_step, n * 4 + 2)
            cast(spl[:, s, 1, :], qk32[:, s, :]).then_inc(spl_step, 1)
            own_wait(pool, spl_step, n * 4 + 3)
            nc.gpsimd.tensor_tensor(qk32[:, s, :], qk32[:, s, :], spl[:, s, 1, :], ALU.subtract).then_inc(spl_step, 1)
            own_wait(pool, spl_step, n * 4 + 4)
            cast(spl[:, s, 2, :], qk32[:, s, :]).then_inc(job_split, 1)

        def pool_split_max(pool, sup, unit):
            s = unit % 2
            n = sup * 16 + unit * 4
            own_wait(pool, nm_ready, sup * 4 + (unit + 1))
            if not (isinstance(sup, int) and sup * 4 + unit < 1):
                own_wait(pool, s_psum, sup * 132 + (rows_at(sup, unit - 1) + 1))
            v = nm[:, s, :].rearrange("p (q h) -> p q h", q=4)
            w = nmr[:, s, :].rearrange("p (q h) -> p q h", q=4)
            cast(nmb[:, :, 0, :], v).then_inc(nm_step, 1)
            own_wait(pool, nm_step, n + 1)
            nc.gpsimd.tensor_tensor(w, v, nmb[:, :, 0, :], ALU.subtract).then_inc(nm_step, 1)
            own_wait(pool, nm_step, n + 2)
            cast(nmb[:, :, 1, :], w).then_inc(nm_step, 1)
            own_wait(pool, nm_step, n + 3)
            nc.gpsimd.tensor_tensor(w, w, nmb[:, :, 1, :], ALU.subtract).then_inc(nm_step, 1)
            own_wait(pool, nm_step, n + 4)
            cast(nmb[:, :, 2, :], w).then_inc(nm_parts, 1)

        def pool_values(pool, sup, set_, batch, group):
            if isinstance(batch, int):
                src = XV[:, 3 - batch, :].rearrange("p (k n) -> p k n", k=KEYT)
            else:
                flat = XV[:, 2:4, :].rearrange("p a n -> p (a n)")
                src = flat[:, bass.ds((1 - batch) * 4096, 4096)].rearrange("p (k n) -> p k n", k=KEYT)
            src = src[:, :, bass.ds(group * P + set_ * 64, 64)].rearrange("p k (h d) -> p k h d", h=GH)
            nc.gpsimd.tensor_copy(Vg[:, set_, :, :, 0:DK], src).then_inc(vg_ready, 1)

        def pool_superunit(pool, sup, batch, group, nbatch, ngroup, last):
            pool_values(pool, sup, 1, batch, group)
            if last:
                own_wait(pool, vg_ready, 2 * SUPERS)
                nc.gpsimd.memset(XV[ILAST:P, 3, 2 * DQ - HID:2 * DQ], 0.0).then_inc(down_zero, 1)
                pool.wait_ge(down_zero, 1)
            for step in range(STEPS):
                if not last and step < 16 and step % 4 == 3:
                    pool_split_job(pool, sup + 1, step // 4)
                if step % KEYT == 4:
                    u = step // KEYT + 1
                    if u < 4:
                        pool_split_max(pool, sup, u)
                    elif not last:
                        pool_split_max(pool, sup + 1, 0)
                if step == 17 and not last:
                    own_wait(pool, av_done, sup * STEPS + 16)
                    pool_values(pool, sup + 1, 0, nbatch, ngroup)
            if not last:
                own_wait(pool, av_done, (sup + 1) * STEPS)

        def pool_att(pool, t, r):
            if isinstance(t, int):
                b, at = t // 8, t % 8 * P
                a, d = num[b][:, :, at:at + P], rdn[:, b, :, at:at + P]
            else:
                b, at = t // 8, (t % 8) * P
                flat = XV[:, 1:3, :].rearrange("p a n -> p (a n)")
                a = flat[:, bass.ds(b * 4096, 4096)].rearrange("p (g t) -> p g t", g=SPB)[:, :, bass.ds(at, P)]
                flat = rdn.rearrange("p b g t -> p (b g t)")
                d = flat[:, bass.ds(b * 4096, 4096)].rearrange("p (g t) -> p g t", g=SPB)[:, :, bass.ds(at, P)]
            if first(t, 1):
                pool.wait_ge(num_in[0], 16)
                pool.wait_ge(rdn_in[0], 64)
                pool.wait_ge(w_tern, 12)
            if first(t, 3) and t == 2:
                pool.wait_ge(num_in[1], 16)
                pool.wait_ge(rdn_in[1], 64)
            if not first(t, 2):
                own_wait(pool, o_psum, t - 1)
            nc.gpsimd.tensor_tensor(att[:, r % 2, :, :], a, d, ALU.mult).then_inc(att_ready, 1)

        def pool_rstd(pool, t, r):
            own_wait(pool, f_stats, t + 1)
            nc.gpsimd.tensor_scalar(vpe[:, r:r + 1], bag[:, r, 1:2], LN_EPS, 1.0, ALU.add, ALU.mult).then_inc(f_var, 1)
            own_wait(pool, f_var, t + 1)
            nc.gpsimd.tensor_tensor(rstd[:, r:r + 1], vpe[:, r:r + 1], expo[:, r:r + 1], ALU.pow).then_inc(f_rs, 1)

        @block.gpsimd
        def _(pool):
            g = nc.gpsimd
            g.memset(ones[:], 1.0).then_inc(consts, 1)
            g.memset(expo[:], -0.5).then_inc(consts, 1)
            g.memset(magic[:], MAGIC).then_inc(consts, 1)
            g.memset(ident[:], 0.0).then_inc(consts, 1)
            g.memset(identb[:], 0.0).then_inc(consts, 1)
            g.memset(Vg[:, :, :, :, :], 1.0).then_inc(consts, 3)
            pool.wait_ge(consts, 8)
            for m in (ident, identb):
                g.affine_select(out=m[:], in_=m[:], compare_op=ALU.not_equal, fill=1.0, base=0,
                                pattern=[[-1, P]], channel_multiplier=1).then_inc(ident_ok, 1)

            def rstds(j):
                own_wait(pool, stats, j + 1)
                if not first(j, 1):
                    own_wait(pool, xn_ready, j * 4)
                g.tensor_scalar(vpe[:], bag[:, :, 1], LN_EPS, 1.0, ALU.add, ALU.mult).then_inc(var_ok, 1)
                own_wait(pool, var_ok, j + 1)
                g.tensor_tensor(rstd[:], vpe[:], expo[:], ALU.pow).then_inc(rs_ready, 1)
            rstds(0)
            rstds(1)
            for job in range(4):
                pool_split_job(pool, 0, job)
            rstds(2)
            pool.wait_ge(w_min, 4)
            pool.wait_ge(rs_ready, 3)
            for s in range(2):
                g.memset(QK[ROWS:AUG, s, 1, :, :], 1.0).then_inc(ones_set, 1)
                pool.wait_ge(ones_set, s + 1)
            rstds(3)
            pool.wait_ge(v_copy, BT)
            pool_values(pool, 0, 0, 0, 0)
            pool.wait_ge(vg_ready, 1)
            pool_split_max(pool, 0, 0)
            pool.wait_ge(v_copy, TILES)
            with pool.Fori(0, SUPERS - 1) as i:
                pool_superunit(pool, i, i // SPB, i % SPB, (i + 1) // SPB, (i + 1) % SPB, False)
            pool_superunit(pool, SUPERS - 1, 1, SPB - 1, 1, 0, True)

            def one(tile):
                stage(tile, 1, lambda t, r: pool_rstd(pool, t, r))
                stage(tile, 2, lambda t, r: pool_att(pool, t, r))
            positions(None, pool, one)

        def sp_parts_out(sp, sup, job):
            qk, half = job // 2, job % 2
            sp.wait_ge(job_split, sup * 4 + (job + 1))
            for part in range(3):
                dst = parts_d[sup, qk, part * DK:(part + 1) * DK, :, half * HALF:(half + 1) * HALF] if isinstance(sup, int) \
                    else parts_d[bass.ds(sup, 1), qk, part * DK:(part + 1) * DK, :, half * HALF:(half + 1) * HALF].rearrange("a d h t -> (a d) h t")
                sp.dma_start(dst.rearrange("d h t -> h d t"), spl[:, job % 2, part, :]).then_inc(parts_out[job % 2], 16)

        def sp_stack(sp, sup, set_):
            for r in range(2):
                sp.wait_ge(parts_out[r], sup * 96 + 96)
            def part(qk, lo, n):
                if isinstance(sup, int):
                    v = parts_d[sup, qk, lo * DK:(lo + n) * DK, set_ * GH:(set_ + 1) * GH, :]
                else:
                    v = parts_d[bass.ds(sup, 1), qk, lo * DK:(lo + n) * DK, set_ * GH:(set_ + 1) * GH, :].rearrange("a d h t -> (a d) h t")
                return v.rearrange("x h t -> x (h t)")
            def rows(qk, a, n):
                return QK[a * DK:(a + n) * DK, set_, qk, :, :].rearrange("x h t -> x (h t)")
            def load(dst, src):
                sp.dma_start(dst, src).then_inc(stack_in[set_], 16)
            load(rows(0, 0, 3), part(0, 0, 3))
            load(rows(1, 0, 3), part(1, 0, 1).unsqueeze(0).broadcast_to([3, DK, GH * SEQ]))
            load(rows(0, 3, 2), part(0, 0, 2))
            load(rows(1, 3, 2), part(1, 1, 1).unsqueeze(0).broadcast_to([2, DK, GH * SEQ]))
            load(rows(0, 5, 1), part(0, 0, 1))
            load(rows(1, 5, 1), part(1, 2, 1))

        def sp_max_rows(sp, sup, unit):
            set_, half = unit // 2, unit % 2
            sp.wait_ge(s_used, sup * 132 + (rows_at(sup, unit) + 1))
            sp.dma_start(QK[ROWS:AUG, set_, 0, :, half * HALF:(half + 1) * HALF], nmT[:, unit % 2, :])\
                .then_inc(nm_in[half], 16)

        def sp_weights(sp, qk, group):
            w = (wqT, wkT)[qk].rearrange("(k p) n -> p k n", p=P)
            sp.dma_start(wqk[:, qk, :, :], w[:, :, bass.ds(group * P, P)]).then_inc((wq_in, wk_in)[qk], 16)

        def sp_sums_out(sp, sup, batch, group, unit):
            gl, half = unit // 2, unit % 2
            if isinstance(sup, int):
                dst = att_d[batch, :, gl * GH:(gl + 1) * GH, group, half * HALF:(half + 1) * HALF]
            else:
                dst = att_d.rearrange("b x h g t -> b g x h t")[bass.ds(batch, 1), bass.ds(group, 1)]\
                    .rearrange("b g x h t -> (b g x) h t")[:, gl * GH:(gl + 1) * GH, half * HALF:(half + 1) * HALF]
            sp.wait_ge(os_copy, sup * 4 + (unit + 2))
            sp.dma_start(dst.rearrange("x h t -> h x t"), OS[:, unit % 2, :]).then_inc(os_out[unit % 2], 16)

        def sp_superunit(sp, sup, batch, group, ngroup2, last):
            sp_stack(sp, sup, 1)
            if last:
                sp_tail_loads(sp)
            if not last:
                sp_parts_out(sp, sup + 1, 0)
            sp_max_rows(sp, sup, 1)
            if not last:
                sp_parts_out(sp, sup + 1, 1)
                sp_weights(sp, 0, ngroup2)
            sp_sums_out(sp, sup, batch, group, 0)
            if not last:
                sp_parts_out(sp, sup + 1, 2)
            sp_max_rows(sp, sup, 2)
            if not last:
                sp_parts_out(sp, sup + 1, 3)
                sp_weights(sp, 1, ngroup2)
            sp_sums_out(sp, sup, batch, group, 1)
            if not last:
                sp.wait_ge(st_psum, sup * (2 * STEPS) + STEPS)
                sp_stack(sp, sup + 1, 0)
            sp_max_rows(sp, sup, 3)
            sp_sums_out(sp, sup, batch, group, 2)
            if not last:
                sp_max_rows(sp, sup + 1, 0)
            sp_sums_out(sp, sup, batch, group, 3)

        def sp_den_in(sp, b):
            sp.dma_start(den[:, b, :], att_d[b, DK, :, :, :].rearrange("h g (c t) -> (h g c) t", t=256))\
                .then_inc(den_in[b], 16)

        def sp_num_in(sp, b):
            sp.dma_start(num[b], att_d[b, 0:DK].rearrange("x h g t -> (x h) g t")).then_inc(num_in[b], 16)

        def sp_tail_loads(sp):
            sp.wait_ge(job_split, 4 * SUPERS)
            sp.wait_ge(vg_ready, 2 * SUPERS)
            sp_down_loads(sp)
            for g in range(SPB):
                sp.dma_start(wo[:, g, :], woT[g * P:(g + 1) * P, :].rearrange("(h d) n -> d h n", d=DK)).then_inc(wo_in, 16)
            for r in range(2):
                sp.wait_ge(os_out[r], 32 * SPB + 16)
            sp_den_in(sp, 0)
            sp_num_in(sp, 0)

        def sp_down_loads(sp):
            w = wdT[0:(IT - 1) * P, :].rearrange("(k p) n -> p k n", p=P)
            half = 2 * DQ
            for s, c0 in ((0, 0), (3, half)):
                k0, off = c0 // HID, c0 % HID
                dst, src_k, c = XV[:, s, 0:half], k0, 0
                if off:
                    sp.dma_start(dst[:, 0:HID - off], w[:, k0, off:HID]).then_inc(raw_in[2], 16)
                    c, src_k = HID - off, k0 + 1
                n = min((half - c) // HID, IT - 1 - src_k)
                sp.dma_start(dst[:, c:c + n * HID].rearrange("p (k n) -> p k n", n=HID), w[:, src_k:src_k + n, :])\
                    .then_inc(raw_in[2], 16)
                c, src_k = c + n * HID, src_k + n
                if src_k < IT - 1:
                    sp.dma_start(dst[:, c:half], w[:, src_k, 0:half - c]).then_inc(raw_in[2], 16)
                else:
                    sp.dma_start(dst[0:ILAST, c:half], wdT[(IT - 1) * P:, :]).then_inc(raw_in[2], 16)

        @block.sync
        def _(sp):
            for r in range(2):
                sp.sem_inc(os_out[r], 16)
                sp.sem_inc(nm_in[r], 16)
            sp.sem_inc(os_copy, 1)
            xt = x.rearrange("(t p) n -> p t n", p=P)

            def tiles(j):
                for r in range(4):
                    if j > 0:
                        sp.wait_ge(xn_ready, j * 4 + (r - 3))
                    sp.dma_start(xin[:, r, :], xt[:, j * 4 + r, :]).then_inc(x_in[r], 16)

            def gate_up(w):
                src, dst = (wgT, wuT)[w], (raw_g, raw_u)[w]
                sp.dma_start(dst.rearrange("p (k n) -> p k n", k=KT), src.rearrange("(k p) n -> p k n", p=P))\
                    .then_inc(raw_in[w], 16)
            tiles(0)
            gate_up(0)
            tiles(1)
            sp_weights(sp, 0, 0)
            sp_weights(sp, 1, 0)
            for n, s in enumerate((s_gate, s_up, s_down)):
                sp.dma_start(srow[0:1, n:n + 1], s.rearrange("(a n) -> a n", a=1)).then_inc(s_in, 16)
            gate_up(1)
            sp.dma_start(wv[:, :, :], wvT.rearrange("(k p) n -> p k n", p=P)).then_inc(wv_in, 16)
            tiles(2)
            for job in range(4):
                sp_parts_out(sp, 0, job)
            sp.wait_ge(w_min, 4)
            sp_stack(sp, 0, 0)
            sp_weights(sp, 0, 1)
            sp_weights(sp, 1, 1)
            tiles(3)
            sp.wait_ge(ones_set, 2)
            sp_max_rows(sp, 0, 0)
            with sp.Fori(0, SUPERS - 1) as i:
                sp_superunit(sp, i, i // SPB, i % SPB, (i + 2) % SPB, False)
            sp_superunit(sp, SUPERS - 1, 1, SPB - 1, 0, True)

            def rden(b):
                sp.wait_ge(den_rec, b + 1)
                sp.dma_start(rden_d[b].rearrange("h g (c t) -> (h g c) t", t=256), den[:, b, :]).then_inc(rden_out, 16)
                sp.wait_ge(rden_out, 16 * b + 16)
                for g in range(SPB):
                    sp.dma_start(rdn[:, b, g, :], rden_d[b, :, g, :].unsqueeze(0).broadcast_to([DK, SH, SEQ]))\
                        .then_inc(rdn_in[b], 16)
            for r in range(2):
                sp.dma_start(xr[:, r, :], xt[:, r, :]).then_inc(xr_in[r], 16)
            rden(0)
            for r in range(2):
                sp.wait_ge(os_out[r], 32 * SUPERS + 16)
            sp_den_in(sp, 1)
            sp_num_in(sp, 1)
            rden(1)
            ot = out.rearrange("(t p) n -> p t n", p=P)

            def one(tile):
                def load(t, r):
                    if first(t, 2):
                        return
                    if not first(t, 4):
                        sp.wait_ge(o_ready, t - 3)
                    if isinstance(t, int):
                        sp.dma_start(xr[:, r, :], xt[:, t, :]).then_inc(xr_in[r], 16)
                    else:
                        sp.dma_start(xr[:, r:r + 1, :], xt[:, bass.ds(t, 1), :]).then_inc(xr_in[r], 16)

                def store(t, r):
                    sp.wait_ge(o_ready, t + 1)
                    if isinstance(t, int):
                        sp.dma_start(ot[:, t, :], outt[:, r % 2, :]).then_inc(out_done[r], 16)
                    else:
                        sp.dma_start(ot[:, bass.ds(t, 1), :], outt[:, r % 2:r % 2 + 1, :]).then_inc(out_done[r], 16)
                stage(tile, 2, load)
                stage(tile, -1, store)
            positions(None, sp, one)
            for r in range(4):
                sp.wait_ge(out_done[r], 4 * TILES)


_WEIGHTS = {"wqT": "L0_attn_w_q", "wkT": "L0_attn_w_k", "wvT": "L0_attn_w_v", "woT": "L0_attn_w_o",
            "wgT": "L0_ffn_w_gate", "wuT": "L0_ffn_w_up", "wdT": "L0_ffn_w_down"}
_SCALES = {"s_gate": "L0_ffn_s_gate", "s_up": "L0_ffn_s_up", "s_down": "L0_ffn_s_down"}


def kernel(**inputs):
    import concourse.bacc as bacc
    from concourse.bass_utils import run_bass_kernel_spmd

    x = np.asarray(inputs["L0_attn_x"])
    arrays = {"x": np.ascontiguousarray(x.reshape(TOK, HID))}
    for name, given in _WEIGHTS.items():
        arrays[name] = np.ascontiguousarray(np.asarray(inputs[given]).T)
    for name, given in _SCALES.items():
        arrays[name] = np.ascontiguousarray(inputs[given])
    nc = bacc.Bacc("TRN2", target_bir_lowering=False, num_devices=1)
    args = {name: nc.dram_tensor(name, a.shape, mybir.dt.from_np(a.dtype), kind="ExternalInput").ap()
            for name, a in arrays.items()}
    out = nc.dram_tensor("out", (TOK, HID), F32, kind="ExternalOutput").ap()
    build(nc, out=out, **args)
    r = run_bass_kernel_spmd(nc, [arrays], core_ids=[0])
    return r.results[0]["out"].reshape(BATCH, SEQ, HID)
```
